# Optimizing a Trainium2 kernel written in Bass

```python
import numpy as np
import jax
import jax.numpy as jnp

def _softmax(x, axis=-1):
    return jax.nn.softmax(x, axis=axis)

def _gelu(x):
    return jax.nn.gelu(x, approximate=True)

def _silu(x):
    return jax.nn.silu(x)

def _sigmoid(x):
    return jax.nn.sigmoid(x)

def _layernorm(x, axis=-1, eps=1e-05):
    m = jnp.mean(x, axis=axis, keepdims=True)
    v = jnp.var(x, axis=axis, keepdims=True)
    return (x - m) / jnp.sqrt(v + eps)

def _scatter_add(tgt, idx, src, axis=0):
    return tgt.at[idx].add(src)

def _segment_sum(src, seg, n):
    return jax.ops.segment_sum(src, seg, n)
kernel_name = 'mk_vit_tower_cls_d1_tok_img2048_r4_5ffa75'

def setup_inputs(seed: int=0):
    np.random.seed(seed)
    _w = jnp.asarray

    def _rec_inputs():
        import jax
        import jax.numpy as jnp
        _rk = jax.random.key(seed)
        x = -0.00340659 + 1.00146 * jax.random.normal(jax.random.fold_in(_rk, 1), (8, 256, 64, 2), jnp.float32)
        cls_tok = 0.02 * jax.random.normal(jax.random.fold_in(_rk, 5), (1, 1, 512), jnp.float32)
        return (x, cls_tok)
    x, cls_tok = _rec_inputs()

    def _L0_tok_setup():
        import jax, jax.numpy as jnp
        import numpy as np
        CH, H, N, N_SSM, SEQ_L = (1, 256, 64, 256, 512)

        def _kernel(C_ri, log_dt, B_ri, inv_A_real, A_imag, L):
            C = C_ri[..., 0] + 1j * C_ri[..., 1]
            B = B_ri[..., 0] + 1j * B_ri[..., 1]
            A = -jnp.exp(inv_A_real) + 1j * A_imag
            rep = log_dt.shape[0] // inv_A_real.shape[0]
            B = jnp.tile(B, (rep, 1))
            A = jnp.tile(A, (rep, 1))
            dt = jnp.exp(log_dt)
            dtA = A * dt[:, None]
            Ct = B[None] * C / (1.0 - dtA / 2) * dt[:, None]
            dA = (1.0 + dtA / 2) / (1.0 - dtA / 2)
            dA_log = jnp.log(dA)
            l = jnp.arange(L, dtype=jnp.float32)
            V = jnp.exp(dA_log[:, :, None] * l)
            K = 2.0 * jnp.einsum('chn,hnl->chl', Ct, V).real
            return K
        key = jax.random.key(seed)
        ks = jax.random.split(key, 5)
        return {'C_ri': jax.random.normal(ks[0], (CH, H, N, 2), dtype=jnp.float32), 'log_dt': jax.random.normal(ks[1], (H,), dtype=jnp.float32), 'B_ri': jax.random.normal(ks[2], (N_SSM, N, 2), dtype=jnp.float32), 'inv_A_real': jax.random.normal(ks[3], (N_SSM, N), dtype=jnp.float32), 'A_imag': jax.random.normal(ks[4], (N_SSM, N), dtype=jnp.float32), 'L': SEQ_L}
    _L0_tok_all = _L0_tok_setup()
    _L0_tok_in = {k: v for k, v in _L0_tok_all.items() if k in ('log_dt', 'B_ri', 'inv_A_real', 'A_imag')}
    del _L0_tok_all

    def _L0_attn_setup():
        import jax, jax.numpy as jnp
        import numpy as np
        NUM_HEADS = 16
        key = jax.random.key(seed)
        k0, k1, k2 = jax.random.split(key, 3)
        B, S, D = (2, 512, 512)
        hd = D // NUM_HEADS
        hidden_states = jax.random.normal(k0, (B, S, D), dtype=jnp.float32)
        c_attn_w = jax.random.normal(k1, (D + 2 * hd, D), dtype=jnp.float32) * 0.02
        c_attn_b = jnp.zeros((D + 2 * hd,), dtype=jnp.float32)
        c_proj_w = jax.random.normal(k2, (D, D), dtype=jnp.float32) * 0.02
        c_proj_b = jnp.zeros((D,), dtype=jnp.float32)
        return {'hidden_states': hidden_states, 'c_attn_w': c_attn_w, 'c_attn_b': c_attn_b, 'c_proj_w': c_proj_w, 'c_proj_b': c_proj_b}
    _L0_attn_all = _L0_attn_setup()
    _L0_attn_in = {k: v for k, v in _L0_attn_all.items() if k in ('c_attn_w', 'c_attn_b', 'c_proj_w', 'c_proj_b')}
    del _L0_attn_all

    def _L0_ffn_setup():
        import jax, jax.numpy as jnp
        import numpy as np
        B, S, D = (2, 512, 512)
        I = 256
        E = 32
        K = 4
        NS = 1
        ALPHA = 7.0

        def _clamped_swiglu(x, wg, wu, wd):
            g = jnp.clip(x @ wg.T, -ALPHA, ALPHA)
            u = jnp.clip(x @ wu.T, -ALPHA, ALPHA)
            return jax.nn.silu(g) * u @ wd.T
        key = jax.random.key(seed)
        ks = jax.random.split(key, 9)
        s = 0.02
        return {'hidden': jax.random.normal(ks[0], (B, S, D), jnp.float32), 'router_w': jax.random.normal(ks[1], (E, D), jnp.float32) * s, 'expert_bias': jax.random.normal(ks[2], (E,), jnp.float32) * s, 'gate_w': jax.random.normal(ks[3], (E, I, D), jnp.float32) * s, 'up_w': jax.random.normal(ks[4], (E, I, D), jnp.float32) * s, 'down_w': jax.random.normal(ks[5], (E, D, I), jnp.float32) * s, 'shared_gate_w': jax.random.normal(ks[6], (NS * I, D), jnp.float32) * s, 'shared_up_w': jax.random.normal(ks[7], (NS * I, D), jnp.float32) * s, 'shared_down_w': jax.random.normal(ks[8], (D, NS * I), jnp.float32) * s}
    _L0_ffn_all = _L0_ffn_setup()
    _L0_ffn_in = {k: v for k, v in _L0_ffn_all.items() if k in ('router_w', 'expert_bias', 'gate_w', 'up_w', 'down_w', 'shared_gate_w', 'shared_up_w', 'shared_down_w')}
    del _L0_ffn_all
    return {'x': x, 'cls_tok': cls_tok, 'L0_tok_log_dt': _L0_tok_in['log_dt'], 'L0_tok_B_ri': _L0_tok_in['B_ri'], 'L0_tok_inv_A_real': _L0_tok_in['inv_A_real'], 'L0_tok_A_imag': _L0_tok_in['A_imag'], 'L0_attn_c_attn_w': _L0_attn_in['c_attn_w'], 'L0_attn_c_attn_b': _L0_attn_in['c_attn_b'], 'L0_attn_c_proj_w': _L0_attn_in['c_proj_w'], 'L0_attn_c_proj_b': _L0_attn_in['c_proj_b'], 'L0_ffn_router_w': _L0_ffn_in['router_w'], 'L0_ffn_expert_bias': _L0_ffn_in['expert_bias'], 'L0_ffn_gate_w': _L0_ffn_in['gate_w'], 'L0_ffn_up_w': _L0_ffn_in['up_w'], 'L0_ffn_down_w': _L0_ffn_in['down_w'], 'L0_ffn_shared_gate_w': _L0_ffn_in['shared_gate_w'], 'L0_ffn_shared_up_w': _L0_ffn_in['shared_up_w'], 'L0_ffn_shared_down_w': _L0_ffn_in['shared_down_w']}

def reference(x, cls_tok, L0_tok_log_dt, L0_tok_B_ri, L0_tok_inv_A_real, L0_tok_A_imag, L0_attn_c_attn_w, L0_attn_c_attn_b, L0_attn_c_proj_w, L0_attn_c_proj_b, L0_ffn_router_w, L0_ffn_expert_bias, L0_ffn_gate_w, L0_ffn_up_w, L0_ffn_down_w, L0_ffn_shared_gate_w, L0_ffn_shared_up_w, L0_ffn_shared_down_w):
    import jax
    import jax.numpy as jnp

    def _L0_tok_ref(C_ri, log_dt, B_ri, inv_A_real, A_imag, L):
        import jax, jax.numpy as jnp
        import numpy as np
        CH, H, N, N_SSM, SEQ_L = (1, 256, 64, 256, 512)

        def _kernel(C_ri, log_dt, B_ri, inv_A_real, A_imag, L):
            C = C_ri[..., 0] + 1j * C_ri[..., 1]
            B = B_ri[..., 0] + 1j * B_ri[..., 1]
            A = -jnp.exp(inv_A_real) + 1j * A_imag
            rep = log_dt.shape[0] // inv_A_real.shape[0]
            B = jnp.tile(B, (rep, 1))
            A = jnp.tile(A, (rep, 1))
            dt = jnp.exp(log_dt)
            dtA = A * dt[:, None]
            Ct = B[None] * C / (1.0 - dtA / 2) * dt[:, None]
            dA = (1.0 + dtA / 2) / (1.0 - dtA / 2)
            dA_log = jnp.log(dA)
            l = jnp.arange(L, dtype=jnp.float32)
            V = jnp.exp(dA_log[:, :, None] * l)
            K = 2.0 * jnp.einsum('chn,hnl->chl', Ct, V).real
            return K
        return _kernel(C_ri, log_dt, B_ri, inv_A_real, A_imag, L)

    def _L0_attn_ref(hidden_states, c_attn_w, c_attn_b, c_proj_w, c_proj_b):
        import jax, jax.numpy as jnp
        import numpy as np
        NUM_HEADS = 16
        B, S, D = hidden_states.shape
        H = NUM_HEADS
        hd = D // H
        scale = hd ** (-0.5)
        qkv = hidden_states @ c_attn_w.T + c_attn_b
        q = qkv[..., :D].reshape(B, S, H, hd)
        k = qkv[..., D:D + hd]
        v = qkv[..., D + hd:]
        scores = jnp.einsum('bqhd,bkd->bhqk', q, k) * scale
        causal = jnp.tril(jnp.ones((S, S), dtype=bool))
        scores = jnp.where(causal, scores, jnp.finfo(scores.dtype).min)
        attn = jax.nn.softmax(scores, axis=-1)
        ctx = jnp.einsum('bhqk,bkd->bqhd', attn, v).reshape(B, S, D)
        out = ctx @ c_proj_w.T + c_proj_b
        return out

    def _L0_ffn_ref(hidden, router_w, expert_bias, gate_w, up_w, down_w, shared_gate_w, shared_up_w, shared_down_w):
        import jax, jax.numpy as jnp
        import numpy as np
        B, S, D = (2, 512, 512)
        I = 256
        E = 32
        K = 4
        NS = 1
        ALPHA = 7.0

        def _clamped_swiglu(x, wg, wu, wd):
            g = jnp.clip(x @ wg.T, -ALPHA, ALPHA)
            u = jnp.clip(x @ wu.T, -ALPHA, ALPHA)
            return jax.nn.silu(g) * u @ wd.T
        Bb, Ss, Dd = hidden.shape
        flat = hidden.reshape(-1, Dd)
        T = flat.shape[0]
        logits = flat @ router_w.T
        scores = jnp.sqrt(jax.nn.softplus(logits))
        _, idx = jax.lax.top_k(scores + expert_bias, K)
        topv = jnp.take_along_axis(scores, idx, axis=1)
        topv = topv / (topv.sum(axis=-1, keepdims=True) + 1e-20)
        probs = jnp.zeros((T, E), flat.dtype).at[jnp.arange(T)[:, None], idx].set(topv)

        def body(acc, xs):
            wg, wu, wd, p = xs
            return (acc + p[:, None] * _clamped_swiglu(flat, wg, wu, wd), None)
        out, _ = jax.lax.scan(body, jnp.zeros_like(flat), (gate_w, up_w, down_w, probs.T))
        out = out + _clamped_swiglu(flat, shared_gate_w, shared_up_w, shared_down_w)
        return out.reshape(Bb, Ss, Dd)
    h = _L0_tok_ref(x, L0_tok_log_dt, L0_tok_B_ri, L0_tok_inv_A_real, L0_tok_A_imag, 512)
    h = jnp.concatenate([jnp.broadcast_to(cls_tok, (h.shape[0], 1, h.shape[2])), h], axis=1)
    h = h + _L0_attn_ref(_layernorm(h, axis=-1), L0_attn_c_attn_w, L0_attn_c_attn_b, L0_attn_c_proj_w, L0_attn_c_proj_b)
    h = h + _L0_ffn_ref(_layernorm(h, axis=-1), L0_ffn_router_w, L0_ffn_expert_bias, L0_ffn_gate_w, L0_ffn_up_w, L0_ffn_down_w, L0_ffn_shared_gate_w, L0_ffn_shared_up_w, L0_ffn_shared_down_w)
    return h

_drawn_inputs = setup_inputs


def setup_inputs(seed=0):
    import zlib

    import numpy as np

    out = dict(_drawn_inputs(seed))
    spreads = {'L0_attn_c_attn_b': (0.0, 0.1), 'L0_attn_c_proj_b': (0.0, 0.1)}
    factors = {'cls_tok': 4.591,
     'L0_ffn_router_w': 4.091,
     'L0_ffn_expert_bias': 8.0,
     'L0_ffn_gate_w': 3.907,
     'L0_ffn_up_w': 3.867,
     'L0_ffn_down_w': 3.874,
     'L0_ffn_shared_gate_w': 2.841,
     'L0_ffn_shared_up_w': 2.854,
     'L0_ffn_shared_down_w': 2.846}
    for name, (base, spread) in spreads.items():
        noise = np.random.default_rng([zlib.crc32(name.encode()), seed]).standard_normal(out[name].shape)
        drawn = base * np.exp(spread * noise) if base else spread * noise
        out[name] = jnp.asarray(drawn.astype(out[name].dtype))
    for name, factor in factors.items():
        out[name] = (out[name] * factor).astype(out[name].dtype)
    return out
```

```python
from contextlib import ExitStack

import numpy as np

import concourse.bass as bass
from concourse import mybir

NCH = 8
SEQ = 512
DM = 512
HD = 32
EPS = 1e-5
NEXP = 32
FF = 256
ALPHA = 7.0
NT = 17
TOKENS = 128 * (NT - 1) + NCH
SLOTS = TOKENS * 4 // 128 + NEXP
NS = SLOTS + 5
WBUF = 4
UN = 4




def exponential(V, done, out, x, t, k, scale):
    ALU = mybir.AluOpType
    ROUND = 1.5 * 2.0 ** 23
    LN2_HI = 0.693359375
    LN2_LO = float(np.log(2.0)) - LN2_HI
    done(V.tensor_scalar(t, x, -88.0, 89.0, ALU.max, ALU.min))
    done(V.tensor_scalar(k, t, float(1 / np.log(2.0)), ROUND, ALU.mult, ALU.add))
    done(V.tensor_scalar(k, k, ROUND, None, ALU.subtract))
    done(V.scalar_tensor_tensor(out=t, in0=k, scalar=-LN2_HI, in1=t, op0=ALU.mult, op1=ALU.add))
    done(V.scalar_tensor_tensor(out=t, in0=k, scalar=-LN2_LO, in1=t, op0=ALU.mult, op1=ALU.add))
    done(V.tensor_scalar(scale, k, 127.0, None, ALU.add))
    done(V.tensor_scalar(scale, scale, 23, None, ALU.logical_shift_left))
    fact = [1.0]
    for n in range(1, 8):
        fact.append(fact[-1] * n)
    done(V.tensor_scalar(k, t, 1 / fact[7], None, ALU.mult))
    for n in range(6, 0, -1):
        done(V.scalar_tensor_tensor(out=k, in0=k, scalar=1 / fact[n], in1=t, op0=ALU.add, op1=ALU.mult))
    done(V.scalar_tensor_tensor(out=out, in0=k, scalar=1.0, in1=scale.bitcast(mybir.dt.float32), op0=ALU.add, op1=ALU.mult))
def ssm_stage(nc, T):
    f32 = mybir.dt.float32
    ALU = mybir.AluOpType
    ACT = mybir.ActivationFunctionType
    NI = 128
    IC = 16
    CHUNKS = NI // IC
    LB = 64
    LA = SEQ // LB
    AC = LA * NCH
    PW = 9
    with ExitStack() as ctx:
        sb = lambda name, shape, dt=f32: ctx.enter_context(nc.sbuf_tensor(name, shape, dt))
        sem = lambda name: ctx.enter_context(nc.semaphore(name))
        par = sb("ssm_par", [128, 5, NI])
        cri = sb("ssm_c", [128, 2, NI * NCH])
        ex = sb("ssm_exp", [128, 2, NI])
        exi = sb("ssm_exp_scale", [128, 2, NI], mybir.dt.int32)
        wk = sb("ssm_work", [128, 10, NI])
        ng = sb("ssm_minus_g", [128, 2, NI])
        z = sb("ssm_z", [128, PW, 2, NI])
        vb = [sb(f"ssm_v{n}", [128, 2, IC, LB]) for n in range(2)]
        qb = [sb(f"ssm_q{n}", [128, 2, IC, AC]) for n in range(2)]
        tv = sb("ssm_tv", [128, 2, 2, IC, LB // 2])
        tq = sb("ssm_tq", [128, 2, 2, IC, AC // 2])
        kb = [sb(f"ssm_k{n}", [128, IC, LB]) for n in range(2)]
        ps = [ctx.enter_context(nc.psum_tensor(f"ssm_ps{n}", [128, IC, LB], f32)) for n in range(2)]
        in_ready = sem("ssm_in_ready")
        dve_step = sem("ssm_dve_step")
        pool_step = sem("ssm_pool_step")
        v_free = [sem(f"ssm_v_free{n}") for n in range(2)]
        q_free = [sem(f"ssm_q_free{n}") for n in range(2)]
        ps_free = [sem(f"ssm_ps_free{n}") for n in range(2)]
        q_ready = sem("ssm_q_ready")
        prod_ready = sem("ssm_prod_ready")
        turn = sem("ssm_turn")
        k_ready = sem("ssm_k_ready")
        k_free = [sem(f"ssm_k_free{n}") for n in range(2)]
        k_stored = [sem(f"ssm_k_stored{n}") for n in range(2)]
        z_steps = []
        block = ctx.enter_context(nc.Block())

        @block.sync
        def _(sp):
            sp.dma_start(par[:, 1:, :], T["ssm_par"]).then_inc(in_ready, 16)
            for p in range(2):
                sp.dma_start(par[64 * p:64 * p + 64, 0, :],
                             T["log_dt"][p:p + 1, :].partition_broadcast(64)).then_inc(in_ready, 16)
            sp.dma_start(cri[:], T["c_ri"]).then_inc(in_ready, 16)
            with sp.Fori(0, CHUNKS // 2) as it:
                for n in range(2):
                    sp.wait_ge(k_ready, it * 2 + n + 1)
                    sp.dma_start(T["hs"][:, bass.ds(it * (2 * IC) + n * IC, IC), :], kb[n][:]).then_inc(k_stored[n], 16)
                    sp.wait_ge(k_stored[n], it * 16 + 16)
                    sp.sem_inc(k_free[n], 1)

        @block.scalar
        def _(act):
            for n in range(2):
                act.sem_inc(k_free[n], 1)
                act.sem_inc(ps_free[n], 1)
            with act.Fori(0, CHUNKS // 2) as it:
                for n in range(2):
                    act.wait_ge(prod_ready, it * 2 + n + 1)
                    act.wait_ge(k_free[n], it + 1)
                    nc.scalar.copy(kb[n][:], ps[n][:]).then_inc(k_ready, 1)
                    act.wait_ge(k_ready, it * 2 + n + 1)
                    act.sem_inc(ps_free[n], 1)

        @block.vector
        def _(dve):
            V = nc.vector
            steps = [0]

            def done(ins):
                steps[0] += 1
                ins.then_inc(dve_step, 1)
                dve.wait_ge(dve_step, steps[0])

            w = lambda k: wk[:, k, :]
            dve.wait_ge(in_ready, 64)
            exponential(V, done, ex[:], par[:, 0:2, :], wk[:, 0:2, :], wk[:, 2:4, :], exi[:])
            dt_, dec = ex[:, 0, :], ex[:, 1, :]
            V.scalar_tensor_tensor(out=w(0), in0=dec, scalar=-0.5, in1=dt_, op0=ALU.mult, op1=ALU.mult)
            done(V.scalar_tensor_tensor(out=w(1), in0=par[:, 2, :], scalar=0.5, in1=dt_, op0=ALU.mult, op1=ALU.mult))
            V.tensor_scalar(w(2), w(0), -1.0, 1.0, ALU.mult, ALU.add)
            V.tensor_tensor(w(3), w(0), w(0), ALU.mult)
            done(V.tensor_tensor(w(4), w(1), w(1), ALU.mult))
            V.tensor_tensor(w(5), w(2), w(2), ALU.mult)
            done(V.tensor_tensor(w(6), w(3), w(4), ALU.add))
            done(V.tensor_tensor(w(5), w(5), w(4), ALU.add))
            done(V.reciprocal(w(7), w(5)))
            V.tensor_scalar(w(6), w(6), -1.0, 1.0, ALU.mult, ALU.add)
            V.scalar_tensor_tensor(out=z[:, 0, 1, :], in0=w(1), scalar=2.0, in1=w(7), op0=ALU.mult, op1=ALU.mult)
            done(V.scalar_tensor_tensor(out=w(8), in0=w(7), scalar=-2.0, in1=dt_, op0=ALU.mult, op1=ALU.mult))
            V.tensor_tensor(z[:, 0, 0, :], w(6), w(7), ALU.mult)
            V.tensor_tensor(w(2), w(2), w(8), ALU.mult)
            done(V.tensor_tensor(w(1), w(1), w(8), ALU.mult))
            V.tensor_tensor(w(3), par[:, 3, :], w(2), ALU.mult)
            V.tensor_tensor(w(4), par[:, 4, :], w(1), ALU.mult)
            V.tensor_tensor(w(5), par[:, 3, :], w(1), ALU.mult)
            done(V.tensor_tensor(w(6), par[:, 4, :], w(2), ALU.mult))
            V.tensor_tensor(ng[:, 0, :], w(3), w(4), ALU.subtract)
            done(V.tensor_tensor(ng[:, 1, :], w(5), w(6), ALU.add))
            for k in range(PW - 1):
                V.tensor_tensor(w(0), z[:, k, 0, :], z[:, k, 0, :], ALU.mult)
                V.tensor_tensor(w(1), z[:, k, 1, :], z[:, k, 1, :], ALU.mult)
                done(V.scalar_tensor_tensor(out=z[:, k + 1, 1, :], in0=z[:, k, 0, :], scalar=2.0, in1=z[:, k, 1, :],
                                            op0=ALU.mult, op1=ALU.mult))
                done(V.tensor_tensor(z[:, k + 1, 0, :], w(0), w(1), ALU.subtract))
            base = steps[0]
            z_steps.append(base)
            per_chunk = 1 + 12
            with dve.Fori(0, CHUNKS // 2) as it:
                for n in range(2):
                    i0 = it * (2 * IC) + n * IC
                    at = lambda s, it=it, n=n: base + (it * 2 + n) * per_chunk + s
                    v, s = vb[n], 1
                    dve.wait_ge(v_free[n], it + 1)
                    V.memset(v[:, 0, :, 0:1], 1.0)
                    V.memset(v[:, 1, :, 0:1], 0.0).then_inc(dve_step, 1)
                    dve.wait_ge(dve_step, at(s))
                    for k in range(6):
                        m = 1 << k
                        old = v[:, :, :, 0:m]
                        for r in range(2):
                            zz = z[:, k, r, bass.ds(i0, IC)].unsqueeze(1).unsqueeze(3).to_broadcast([128, 2, IC, m])
                            last = V.tensor_tensor(tv[:, r, :, :, 0:m], old, zz, ALU.mult)
                        s += 1
                        last.then_inc(dve_step, 1)
                        dve.wait_ge(dve_step, at(s))
                        V.tensor_tensor(v[:, 0, :, m:2 * m], tv[:, 0, 0, :, 0:m], tv[:, 1, 1, :, 0:m], ALU.subtract)
                        s += 1
                        V.tensor_tensor(v[:, 1, :, m:2 * m], tv[:, 0, 1, :, 0:m], tv[:, 1, 0, :, 0:m],
                                        ALU.add).then_inc(dve_step, 1)
                        dve.wait_ge(dve_step, at(s))

        @block.gpsimd
        def _(pool):
            P = nc.gpsimd
            per_chunk = 3 + 2 * 3
            pool.wait_ge(dve_step, z_steps[0])
            with pool.Fori(0, CHUNKS // 2) as it:
                for n in range(2):
                    i0 = it * (2 * IC) + n * IC
                    at = lambda s, it=it, n=n: (it * 2 + n) * per_chunk + s
                    q, s = qb[n], 1
                    c = cri[:].rearrange("p r (i c) -> p r i c", c=NCH)
                    pool.wait_ge(q_free[n], it + 1)
                    for r in range(2):
                        gg = ng[:, r, bass.ds(i0, IC)].unsqueeze(1).unsqueeze(3).to_broadcast([128, 2, IC, NCH])
                        last = P.tensor_tensor(tq[:, r, :, :, 0:NCH], c[:, :, bass.ds(i0, IC), :], gg, ALU.mult)
                    last.then_inc(pool_step, 1)
                    pool.wait_ge(pool_step, at(s))
                    P.tensor_tensor(q[:, 0, :, 0:NCH], tq[:, 1, 1, :, 0:NCH], tq[:, 0, 0, :, 0:NCH], ALU.subtract)
                    s += 1
                    P.tensor_tensor(q[:, 1, :, 0:NCH], tq[:, 0, 1, :, 0:NCH], tq[:, 1, 0, :, 0:NCH],
                                    ALU.add).then_inc(pool_step, 1)
                    pool.wait_ge(pool_step, at(s))
                    for k in range(3):
                        m = NCH << k
                        old = q[:, :, :, 0:m]
                        for r in range(2):
                            zz = z[:, 6 + k, r, bass.ds(i0, IC)].unsqueeze(1).unsqueeze(3).to_broadcast([128, 2, IC, m])
                            last = P.tensor_tensor(tq[:, r, :, :, 0:m], old, zz, ALU.mult)
                        s += 1
                        last.then_inc(pool_step, 1)
                        pool.wait_ge(pool_step, at(s))
                        P.tensor_tensor(q[:, 0, :, m:2 * m], tq[:, 0, 0, :, 0:m], tq[:, 1, 1, :, 0:m], ALU.add)
                        s += 1
                        P.tensor_tensor(q[:, 1, :, m:2 * m], tq[:, 0, 1, :, 0:m], tq[:, 1, 0, :, 0:m],
                                        ALU.subtract).then_inc(pool_step, 1)
                        pool.wait_ge(pool_step, at(s))
                    pool.sem_inc(pool_step, 1)

        @block.tensor
        def _(pe):
            base, v_chunk, q_chunk = z_steps[0], 13, 9
            for n in range(2):
                pe.sem_inc(v_free[n], 1)
                pe.sem_inc(q_free[n], 1)
            with pe.Fori(0, CHUNKS // 2) as it:
                for n in range(2):
                    pe.wait_ge(dve_step, it * (2 * v_chunk) + base + (n + 1) * v_chunk)
                    pe.wait_ge(pool_step, it * (2 * q_chunk) + (n + 1) * q_chunk)
                    pe.wait_ge(ps_free[n], it + 1)
                    pe.sem_inc(turn, 1)
                    for i in range(IC):
                        for p in range(2):
                            h = slice(64 * p, 64 * p + 64)
                            for r in range(2):
                                last = nc.tensor.matmul(ps[n][h, i, :], qb[n][h, r, i, :], vb[n][h, r, i, :],
                                                        start=(r == 0), stop=(r == 1))
                    last.then_inc(prod_ready, 1)
                    pe.wait_ge(prod_ready, it * 2 + n + 1)
                    pe.sem_inc(v_free[n], 1)
                    pe.sem_inc(q_free[n], 1)


def attention_stage(nc, T, H):
    f32, bf16, fr = mybir.dt.float32, mybir.dt.bfloat16, mybir.dt.float32r
    ALU, ACT, AX = mybir.AluOpType, mybir.ActivationFunctionType, mybir.AxisListType
    KC = DM // 128
    NB = 4
    STEPS = 2 * NB
    ITERS = NCH // NB
    GROUPS = 4 * STEPS
    NK = 1 + 2 * 128
    CLS = 2 * NCH
    SCALE = float(HD) ** -0.5

    def tp_order():
        for n in range(STEPS):
            if n % 2 == 0:
                yield from (("x", n // 2, 0), ("x", n // 2, 1), ("v", n // 2, 0))
            for j in range(4):
                g = 4 * n + j - 1
                if g >= 0:
                    yield from (("p", g, kc) for kc in range(1 + (g // 4) % 2))
                if j == 1 and n > 0:
                    yield ("r", n - 1, 0)
        yield from (("p", GROUPS - 1, 0), ("p", GROUPS - 1, 1), ("r", STEPS - 1, 0))

    TP = {use: k for k, use in enumerate(tp_order())}
    TP_USES = len(TP) // 2
    assert len(TP) % 2 == 0

    def qk_order():
        for n in range(STEPS):
            if n % 2 == 0:
                yield from (("qkv", n // 2, m) for m in range(6))
            if n > 0:
                yield from (("rb", n - 1, 0), ("pr", n - 1, 0))
        yield from (("rb", STEPS - 1, 0), ("pr", STEPS - 1, 0))

    QK = {use: k for k, use in enumerate(qk_order())}
    QK_USES = len(QK)

    with ExitStack() as ctx:
        sb = lambda name, shape, dt=f32: ctx.enter_context(nc.sbuf_tensor("at_" + name, shape, dt))
        pb = lambda name, shape, dt=f32: ctx.enter_context(nc.psum_tensor("at_" + name, shape, dt))
        sem = lambda name: ctx.enter_context(nc.semaphore("at_" + name))
        watt = sb("watt", [128, KC, 6 * 128])
        wo = sb("wo", [128, KC, DM])
        bias = sb("bias", [128, 6])
        bo = sb("bo", [128, DM])
        ident = sb("ident", [128, 128])
        identb = sb("identb", [128, 128], bf16)
        maskf = sb("maskf", [128, 128])
        maskb = sb("maskb", [128, 128], bf16)
        selh = sb("selh", [128, 4, 128])
        selv = sb("selv", [128, 4, 128])
        power = sb("power", [128, 1])
        st6 = sb("st6", [128, NT, 6])
        mv = sb("mv", [128, NT, 2])
        ve = sb("ve", [128, NT])
        rstd = sb("rstd", [128, NT])
        xn = sb("xn", [128, 2, DM])
        wh, wl = sb("wh", [128, KC, 6 * 128], fr), sb("wl", [128, KC, 6 * 128], fr)
        oh, ol = sb("oh", [128, KC, DM], fr), sb("ol", [128, KC, DM], fr)
        xh, xl = sb("xh", [128, KC, 256], fr), sb("xl", [128, KC, 256], fr)
        qh, ql = sb("qh", [128, 2, 4, 128], fr), sb("ql", [128, 2, 4, 128], fr)
        kh, kl = sb("kh", [128, 2, 4, NK + 1], fr), sb("kl", [128, 2, 4, NK + 1], fr)
        kp = sb("kp", [128, 2, NK + 1], fr)
        quad = sb("quad", [128, 4])
        kz = sb("kz", [128, 2, 4, 1 + 128])
        ch, cl = sb("ch", [128, 512], fr), sb("cl", [128, 512], fr)
        xT = sb("xT", [128, KC, 128])
        qT = sb("qT", [128, 2, 4, 256])
        kT = sb("kT", [128, 2, NK + 1])
        vT = sb("vT", [128, 256])
        vtok = sb("vtok", [128, 2, 2, HD])
        v0 = sb("v0", [128, 128])
        nmax = sb("nmax", [128, 4])
        pg = sb("pg", [128, 2, 4, NK])
        pt = sb("pt", [128, 4, 3, 512])
        r2 = sb("r2", [128, 2, 128])
        rp = sb("rp", [128, 2, 128])
        rb = sb("rb", [128, 512])
        ctxT = sb("ctxT", [128, 512])
        S = [pb(f"S{m}", [128, 512]) for m in range(4)]
        tp = [pb(f"tp{k}", [128, 512]) for k in range(2)]
        qk = pb("qk", [128, 512])
        cx = pb("cx", [128, 512])
        banks = (qk, cx)
        w_ready, const_ready, h_ready = sem("w_ready"), sem("const_ready"), sem("h_ready")
        dve_step, act_step, pool_step = sem("dve_step"), sem("act_step"), sem("pool_step")
        var_ready, rstd_ready = sem("var_ready"), sem("rstd_ready")
        xn_ready, xn_free = sem("xn_ready"), sem("xn_free")
        hb_ready = sem("hb_ready")
        tp_full = [sem(f"tp_full{k}") for k in range(2)]
        tp_free = [sem(f"tp_free{k}") for k in range(2)]
        qk_full, qk_free = sem("qk_full"), sem("qk_free")
        sc_full, max_done, exp_done = sem("sc_full"), sem("max_done"), sem("exp_done")
        pg_read, p0_done = sem("pg_read"), sem("p0_done")
        rec_ready, rb_ready = sem("rec_ready"), sem("rb_ready")
        pv_done, ctx_ready = sem("pv_done"), sem("ctx_ready")
        wh_ready, wl_ready, xh_ready = sem("wh_ready"), sem("wl_ready"), sem("xh_ready")
        high_ready, keys_ready, ch_ready, ctx_split = sem("high_ready"), sem("keys_ready"), sem("ch_ready"), sem("ctx_split")
        stats, aggr = sem("stats"), sem("aggr")
        load = [sem(f"load{k}") for k in range(4)]
        tile_ready = sem("tile_ready")
        cls_step = sem("cls_step")
        turn, dve_turn, pool_turn = sem("turn"), sem("dve_turn"), sem("pool_turn")

        def transposed(it, use):
            k = TP[use]
            return k % 2, it * TP_USES + k // 2 + 1

        with nc.Block() as block:

            @block.sync
            def _(sp):
                sp.dma_start(ident[:], T["ident"]).then_inc(const_ready, 16)
                sp.dma_start(maskf[:], T["mask"]).then_inc(const_ready, 16)
                sp.dma_start(selh[:], T["selh"]).then_inc(const_ready, 16)
                sp.dma_start(selv[:], T["selv"]).then_inc(const_ready, 16)
                sp.dma_start(quad[:], T["quad"]).then_inc(const_ready, 16)
                sp.dma_start(H[:, CLS, :], T["cls"].partition_broadcast(128)).then_inc(h_ready, 16)
                sp.dma_start(watt[:], T["watt"]).then_inc(w_ready, 16)
                sp.dma_start(bias[:], T["battn"]).then_inc(w_ready, 16)
                sp.dma_start(wo[:], T["wo"]).then_inc(w_ready, 16)
                sp.dma_start(bo[:], T["bo"].partition_broadcast(128)).then_inc(w_ready, 16)
                for t in range(2 * NCH):
                    c, p = t // 2, t % 2
                    src = T["hs"].rearrange("(p a c) i b -> p c i a b", p=2, c=NCH)[p, c]
                    dst = H[:, t, :].rearrange("i (a b) -> i a b", b=src.shape[2])
                    if t >= 4:
                        sp.wait_ge(load[t % 4], 16 * (t // 4))
                        sp.sem_inc(tile_ready, 1)
                    sp.dma_start(dst, src).then_inc(load[t % 4], 16)
                for n in range(4):
                    sp.wait_ge(load[n], 16 * NCH // 2)
                    sp.sem_inc(tile_ready, 1)
                sp.wait_ge(w_ready, 64)

            @block.tensor
            def _(pe):
                pe.wait_ge(const_ready, 80)
                pe.wait_ge(xn_ready, 1)
                for kc in range(KC):
                    last = nc.tensor.transpose(tp[0][:, kc * 128:(kc + 1) * 128], xn[:, 0, kc * 128:(kc + 1) * 128], ident[:])
                last.then_inc(cls_step, 1)
                pe.wait_ge(act_step, 1)
                pe.wait_ge(w_ready, 64)
                for m in (4, 5):
                    for kc in range(KC):
                        last = nc.tensor.matmul(qk[:, (m - 4) * 128:(m - 3) * 128], watt[:, kc, m * 128:(m + 1) * 128],
                                                xT[:, kc, 0:128], start=(kc == 0), stop=(kc == KC - 1))
                last.then_inc(cls_step, 1)
                pe.wait_ge(act_step, 3)
                nc.tensor.transpose(tp[0][:, 0:128], v0[:], ident[:]).then_inc(cls_step, 1)
                for g in range(4):
                    last = nc.tensor.matmul(qk[:], v0[:], wo[:, g, :], start=(g == 0), stop=(g == 3))
                last.then_inc(cls_step, 1)
                pe.wait_ge(dve_step, 4)
                pe.wait_ge(wl_ready, 2)
                with pe.Fori(0, ITERS) as it:
                    def project_in(b):
                        for p in range(2):
                            bank, uses = transposed(it, ("x", b, p))
                            pe.wait_ge(xn_ready, it * (2 * NB) + 2 * b + p + 2)
                            pe.wait_ge(tp_free[bank], uses)
                            for kc in range(KC):
                                last = nc.tensor.transpose(tp[bank][:, kc * 128:(kc + 1) * 128],
                                                           xn[:, p, kc * 128:(kc + 1) * 128], ident[:])
                            last.then_inc(tp_full[bank], 1)
                        for p in range(2):
                            bank, uses = transposed(it, ("x", b, p))
                            pe.wait_ge(tp_free[bank], uses + 1)
                        pe.wait_ge(ctx_ready, it * STEPS + 2 * b + (1 if b == 0 else 0))
                        for m in range(6):
                            pe.wait_ge(qk_free, it * QK_USES + QK[("qkv", b, m)] + (1 if m == 0 else 0) + 1)
                            for kc in range(KC):
                                for w_, x_ in ((wh, xh), (wh, xl), (wl, xh)):
                                    last = nc.tensor.matmul(banks[m % 2][:, 0:256],
                                                            w_[:, kc, m * 128:(m + 1) * 128], x_[:, kc, :],
                                                            start=(kc == 0 and x_ is xh and w_ is wh),
                                                            stop=(kc == KC - 1 and w_ is wl))
                            last.then_inc(qk_full, 1)
                        bank, uses = transposed(it, ("v", b, 0))
                        pe.wait_ge(qk_free, it * QK_USES + QK[("qkv", b, 5)] + 3)
                        pe.wait_ge(tp_free[bank], uses)
                        for p in range(2):
                            last = nc.tensor.transpose(tp[bank][:, 128 * p:128 * p + 128],
                                                       vT[:, 128 * p:128 * p + 128], ident[:])
                        last.then_inc(tp_full[bank], 1)

                    def scores(n, j):
                        b, p, g = n // 2, n % 2, 4 * n + j
                        for m in range(4):
                            pe.wait_ge(exp_done, it * (4 * GROUPS) + 4 * g + m + 1)
                            if p == 1 and j == 0 and m == 0:
                                pe.wait_ge(keys_ready, it * (2 * NB) + 2 * b + 2)
                            pe.sem_inc(turn, 1)
                            keys = 129 if p == 0 else NK
                            if p == 0:
                                nc.tensor.matmul(S[m][:, 0:keys], qT[:, b % 2, m, 0:128], kz[:, b % 2, j, :],
                                                 start=True, stop=False, skip_group_check=True)
                            else:
                                for q_, k_ in ((qh, kh), (qh, kl), (ql, kh)):
                                    nc.tensor.matmul(S[m][:, 0:keys + 1], q_[:, b % 2, m, :], k_[:, b % 2, j, :],
                                                     start=(q_ is qh and k_ is kh), stop=False, skip_group_check=True)
                            nc.tensor.matmul(S[m][:, keys - 128:keys], identb[:], maskb[:], start=False, stop=True,
                                             skip_group_check=True).then_inc(sc_full, 1)

                    def transpose_probs(g):
                        n, j = divmod(g, 4)
                        pe.wait_ge(exp_done, it * (4 * GROUPS) + 4 * g + 8)
                        for kc in range(1 + n % 2):
                            bank, uses = transposed(it, ("p", g, kc))
                            pe.wait_ge(tp_free[bank], uses)
                            for m in range(4):
                                last = nc.tensor.transpose(tp[bank][:, m * 128:(m + 1) * 128],
                                                           pg[:, g % 2, m, 1 + 128 * kc:129 + 128 * kc], ident[:])
                            last.then_inc(tp_full[bank], 1)
                        pe.wait_ge(tp_full[bank], uses)
                        pe.sem_inc(pg_read, 1)

                    def context(n):
                        b, p = n // 2, n % 2
                        bank, uses = transposed(it, ("r", n, 0))
                        pe.wait_ge(rec_ready, it * STEPS + n + 1)
                        pe.wait_ge(p0_done, it * GROUPS + 4 * n + 6)
                        pe.wait_ge(tp_free[bank], uses)
                        pe.sem_inc(turn, 1)
                        nc.tensor.transpose(tp[bank][:, 0:128], r2[:, n % 2, :], ident[:]).then_inc(tp_full[bank], 1)
                        for k in range(2):
                            last = max(TP[("p", 4 * n + j, kc)] for j in range(4) for kc in range(1 + p)
                                       if TP[("p", 4 * n + j, kc)] % 2 == k)
                            pe.wait_ge(tp_free[k], it * TP_USES + last // 2 + 2)
                        pe.wait_ge(ctx_ready, it * STEPS + n + 1)
                        pe.sem_inc(turn, 1)
                        for kc in range(1 + p):
                            for j in range(4):
                                nc.tensor.matmul(cx[32 * j:32 * j + 32, :], vtok[:, b % 2, kc, :], pt[:, j, n % 2 + kc, :],
                                                 start=(kc == 0), stop=False, skip_group_check=True)
                        pe.wait_ge(tp_free[bank], uses + 1)
                        pe.wait_ge(qk_free, it * QK_USES + QK[("rb", n, 0)] + 2)
                        pe.sem_inc(turn, 1)
                        for m in range(4):
                            last = nc.tensor.matmul(cx[:, m * 128:(m + 1) * 128], selv[:, m, :], rp[:, n % 2, :],
                                                    start=False, stop=True, skip_group_check=True)
                        last.then_inc(pv_done, 1)
                        for m in range(4):
                            last = nc.tensor.matmul(qk[:, m * 128:(m + 1) * 128], selh[:, m, :], rp[:, n % 2, :],
                                                    start=(m == 0), stop=True, skip_group_check=True)
                        last.then_inc(qk_full, 1)

                    def project_out(n):
                        pe.wait_ge(ctx_split, it * STEPS + n + 2)
                        pe.wait_ge(qk_free, it * QK_USES + QK[("pr", n, 0)] + 2)
                        pe.sem_inc(turn, 1)
                        for m in range(4):
                            for c_, o_ in ((ch, oh), (ch, ol), (cl, oh)):
                                last = nc.tensor.matmul(qk[:], c_[:, m * 128:(m + 1) * 128], o_[:, m, :],
                                                        start=(m == 0 and c_ is ch and o_ is oh), stop=(m == 3 and c_ is cl))
                        last.then_inc(qk_full, 1)

                    for n in range(STEPS):
                        if n % 2 == 0:
                            project_in(n // 2)
                        for j in range(4):
                            scores(n, j)
                            if 4 * n + j > 0:
                                transpose_probs(4 * n + j - 1)
                            if j == 1 and n > 0:
                                context(n - 1)
                            if j == 3 and n > 0:
                                project_out(n - 1)
                    transpose_probs(GROUPS - 1)
                    context(STEPS - 1)
                    project_out(STEPS - 1)

            @block.scalar
            def _(act):
                A = nc.scalar
                act.wait_ge(w_ready, 64)
                A.copy(wh[:], watt[:]).then_inc(wh_ready, 1)
                A.copy(oh[:], wo[:]).then_inc(wh_ready, 1)
                act.wait_ge(cls_step, 1)
                A.copy(xT[:], tp[0][:].rearrange("p (k t) -> p k t", k=KC)).then_inc(act_step, 1)
                act.wait_ge(cls_step, 2)
                act.wait_ge(pool_step, 2)
                act.wait_ge(dve_step, 1)
                for b in range(2):
                    for j in range(4):
                        rows = slice(32 * j, 32 * j + 32)
                        A.activation(kz[rows, b, j, 0:1], qk[rows, 0:1], ACT.Identity, bias=bias[rows, 4:5])
                A.activation(kT[:, 0, 0:1], qk[:, 0:1], ACT.Identity, bias=bias[:, 4:5])
                A.activation(kT[:, 1, 0:1], qk[:, 0:1], ACT.Identity, bias=bias[:, 4:5]).then_inc(act_step, 1)
                A.activation(v0[:], qk[:, 128:256], ACT.Identity, bias=bias[:, 5:6]).then_inc(act_step, 1)
                act.wait_ge(dve_step, 4)
                act.sem_inc(tp_free[0], 1)
                act.sem_inc(exp_done, 4)
                with act.Fori(0, ITERS) as it:
                    def evacuate(use, dst, view, *waits):
                        bank, uses = transposed(it, use)
                        if bank == 0:
                            act.wait_ge(tp_full[0], uses)
                            A.copy(dst, view(tp[0])).then_inc(tp_free[0], 1)

                    def project_in(b):
                        for p in range(2):
                            bank, uses = transposed(it, ("x", b, p))
                            act.wait_ge(tp_full[bank], uses)
                            A.copy(xh[:, :, 128 * p:128 * p + 128],
                                   tp[bank][:].rearrange("p (k t) -> p k t", k=KC)).then_inc(xh_ready, 1)
                        for m in range(6):
                            act.wait_ge(qk_full, it * QK_USES + QK[("qkv", b, m)] + 1)
                            src = banks[m % 2][:, 0:256]
                            if m == 0:
                                act.wait_ge(pv_done, it * STEPS + 2 * b + 1)
                            if m == 4:
                                for j in range(4):
                                    rows = slice(32 * j, 32 * j + 32)
                                    A.activation(kz[rows, b % 2, j, 1:], banks[m % 2][rows, 0:128], ACT.Identity, bias=bias[rows, 4:5])
                            if m < 4:
                                A.activation(qT[:, b % 2, m, :], src, ACT.Identity, bias=bias[:, m:m + 1],
                                             scale=SCALE).then_inc(qk_free, 1)
                            else:
                                dst = kT[:, b % 2, 1:NK] if m == 4 else vT[:]
                                A.activation(dst, src, ACT.Identity, bias=bias[:, m:m + 1]).then_inc(qk_free, 1)
                        evacuate(("v", b, 0), vtok[:, b % 2], lambda t: t[:, 0:256].rearrange("p (k d) -> p k d", k=2)[:, :, 0:HD])

                    def probs(n, j):
                        g = 4 * n + j
                        act.wait_ge(pg_read, it * GROUPS + g + 1)
                        act.wait_ge(p0_done, it * GROUPS + g + 1)
                        for m in range(4):
                            keys = 129 if n % 2 == 0 else NK
                            act.wait_ge(max_done, it * (4 * GROUPS) + 4 * g + m + 1)
                            if m == 0 and j == 0:
                                act.wait_ge(pv_done, it * STEPS + n + 1)
                            A.activation(pg[:, g % 2, m, 0:keys], S[m][:, 0:keys], ACT.Exp, bias=nmax[:, m:m + 1],
                                         accum_out=r2[:, n % 2, 4 * j + m:4 * j + m + 1]).then_inc(exp_done, 1)

                    def take_probs(g):
                        n, j = divmod(g, 4)
                        for kc in range(1 + n % 2):
                            if j == 0 and kc == 0:
                                act.wait_ge(pv_done, it * STEPS + n + 1)
                            evacuate(("p", g, kc), pt[:, j, n % 2 + kc, :], lambda t: t[:])

                    def context(n):
                        evacuate(("r", n, 0), rp[:, n % 2, :], lambda t: t[:, 0:128])
                        act.wait_ge(qk_full, it * QK_USES + QK[("rb", n, 0)] + 1)
                        act.wait_ge(ctx_ready, it * STEPS + n + 1)
                        A.copy(rb[:], qk[:]).then_inc(qk_free, 1)

                    def split_context(n):
                        act.wait_ge(ctx_ready, it * STEPS + n + 2)
                        A.copy(ch[:], ctxT[:]).then_inc(ch_ready, 1)

                    for n in range(STEPS):
                        if n % 2 == 0:
                            project_in(n // 2)
                        for j in range(4):
                            probs(n, j)
                            if 4 * n + j > 0:
                                take_probs(4 * n + j - 1)
                            if j == 1 and n > 0:
                                context(n - 1)
                            if j == 2 and n > 0:
                                split_context(n - 1)
                    take_probs(GROUPS - 1)
                    context(STEPS - 1)
                    split_context(STEPS - 1)

            @block.vector
            def _(dve):
                V = nc.vector
                dve.wait_ge(const_ready, 80)
                V.tensor_copy(identb[:], ident[:])
                V.tensor_copy(maskb[:], maskf[:])
                V.memset(r2[:], 0.0)
                V.memset(kT[:, :, NK:], 0.0)
                V.memset(kz[:], 0.0)
                V.memset(power[:], -0.5).then_inc(dve_step, 1)

                def statistics(tiles):
                    for t in tiles:
                        if t != CLS:
                            dve.wait_ge(tile_ready, t + 1)
                        V.bn_stats(st6[:, t, :], H[:, t, :]).then_inc(stats, 1)
                    dve.wait_ge(stats, 1 if tiles[0] == CLS else 1 + len(tiles))
                    for t in tiles:
                        V.bn_aggr(mv[:, t, :], st6[:, t, :]).then_inc(aggr, 1)
                    dve.wait_ge(aggr, 1 if tiles[0] == CLS else 1 + len(tiles))
                    r = slice(tiles[0], tiles[-1] + 1)
                    V.tensor_scalar(ve[:, r], mv[:, r, 1], 1.0, EPS, ALU.mult, ALU.add).then_inc(var_ready, 1)

                def normalize(p, h, m, r):
                    V.tensor_scalar(xn[:, p, :], h, m, r, ALU.subtract, ALU.mult).then_inc(xn_ready, 1)

                dve.wait_ge(h_ready, 16)
                statistics([CLS])
                dve.wait_ge(rstd_ready, 1)
                normalize(0, H[:, CLS, :], mv[:, CLS, 0:1], rstd[:, CLS:CLS + 1])
                statistics(range(CLS))
                dve.wait_ge(wh_ready, 1)
                V.tensor_tensor(wl[:], watt[:], wh[:].bitcast(f32), ALU.subtract).then_inc(wl_ready, 1)
                dve.wait_ge(cls_step, 3)
                V.tensor_tensor(selv[32:48], selv[32:48], tp[0][32:48, 0:128].unsqueeze(1).to_broadcast([16, 4, 128]),
                                ALU.mult).then_inc(dve_step, 1)
                dve.wait_ge(cls_step, 4)
                dve.wait_ge(w_ready, 64)
                V.tensor_tensor(H[:, CLS, :], H[:, CLS, :], bo[:], ALU.add).then_inc(dve_step, 1)
                dve.wait_ge(dve_step, 3)
                V.tensor_tensor(H[:, CLS, :], H[:, CLS, :], qk[:], ALU.add).then_inc(dve_step, 1)
                dve.sem_inc(tp_free[1], 1)
                dve.wait_ge(dve_step, 4)
                dve.wait_ge(rstd_ready, 2)
                dve.sem_inc(qk_free, 2)
                dve.sem_inc(ctx_ready, 1)
                with dve.Fori(0, ITERS) as it:
                    def evacuate(use, dst, view):
                        bank, uses = transposed(it, use)
                        if bank == 1:
                            dve.wait_ge(tp_full[1], uses)
                            V.tensor_copy(dst, view(tp[1])).then_inc(tp_free[1], 1)

                    def rows(b):
                        for p in range(2):
                            k = it * (2 * NB) + 2 * b + p
                            if b == 0:
                                dve.wait_ge(cls_step, 1)
                            else:
                                bank, uses = transposed(it, ("x", b - 1, p))
                                dve.wait_ge(tp_full[bank], uses)
                            dve.sem_inc(dve_turn, 1)
                            normalize(p, H[:, bass.ds(k, 1), :].rearrange("q o d -> q (o d)"),
                                      mv[:, bass.ds(k, 1), 0], rstd[:, bass.ds(k, 1)])

                    def first_column(g):
                        n, j = divmod(g, 4)
                        if j == 0:
                            dve.wait_ge(pv_done, it * STEPS + n + 1)
                        dve.wait_ge(exp_done, it * (4 * GROUPS) + 4 * g + 8)
                        dve.sem_inc(dve_turn, 1)
                        V.tensor_copy(r2[:, n % 2, 32 + 4 * j:36 + 4 * j],
                                      pg[:, g % 2, :, 0:1].rearrange("q m o -> q (m o)")).then_inc(p0_done, 1)

                    def project_in(b):
                        for p in range(2):
                            bank, uses = transposed(it, ("x", b, p))
                            dve.wait_ge(xh_ready, it * (2 * NB) + 2 * b + p + 1)
                            part = xh[:, :, 128 * p:128 * p + 128]
                            V.tensor_tensor(xl[:, :, 128 * p:128 * p + 128],
                                            tp[bank][:].rearrange("p (k t) -> p k t", k=KC), part.bitcast(f32),
                                            ALU.subtract).then_inc(tp_free[bank], 1)
                        evacuate(("v", b, 0), vtok[:, b % 2], lambda t: t[:, 0:256].rearrange("p (k d) -> p k d", k=2)[:, :, 0:HD])

                    def maxima(n, j):
                        g = 4 * n + j
                        for m in range(4):
                            keys = 129 if n % 2 == 0 else NK
                            dve.wait_ge(sc_full, it * (4 * GROUPS) + 4 * g + m + 1)
                            dve.wait_ge(exp_done, it * (4 * GROUPS) + 4 * g + m + 1)
                            V.tensor_reduce(out=nmax[:, m:m + 1], in_=S[m][:, 0:keys], axis=AX.X, op=ALU.max,
                                            negate=True).then_inc(max_done, 1)

                    def take_probs(g):
                        n, j = divmod(g, 4)
                        for kc in range(1 + n % 2):
                            if j == 0:
                                dve.wait_ge(pv_done, it * STEPS + n + 1)
                            evacuate(("p", g, kc), pt[:, j, n % 2 + kc, :], lambda t: t[:])

                    def reciprocals(n):
                        dve.wait_ge(exp_done, it * (4 * GROUPS) + 16 * n + 16 + 4)
                        V.reciprocal(r2[:, n % 2, 0:16], r2[:, n % 2, 0:16]).then_inc(rec_ready, 1)

                    def context(n):
                        evacuate(("r", n, 0), rp[:, n % 2, :], lambda t: t[:, 0:128])
                        dve.wait_ge(qk_free, it * QK_USES + QK[("rb", n, 0)] + 3)
                        dve.wait_ge(pv_done, it * STEPS + n + 3)
                        V.tensor_tensor(ctxT[:], cx[:], rb[:], ALU.mult).then_inc(ctx_ready, 1)

                    def split_context(n):
                        dve.wait_ge(ch_ready, it * STEPS + n + 1)
                        dve.sem_inc(dve_turn, 1)
                        V.tensor_tensor(cl[:], ctxT[:], ch[:].bitcast(f32), ALU.subtract).then_inc(ctx_split, 1)

                    def project_out(n):
                        k = it * STEPS + n
                        dve.wait_ge(qk_full, it * QK_USES + QK[("pr", n, 0)] + 1)
                        dve.wait_ge(hb_ready, k + 1)
                        h = H[:, bass.ds(k, 1), :].rearrange("q o d -> q (o d)")
                        V.tensor_tensor(h, h, qk[:], ALU.add).then_inc(qk_free, 1)

                    rows(0)
                    for n in range(STEPS):
                        if n % 2 == 0:
                            project_in(n // 2)
                        for j in range(4):
                            maxima(n, j)
                            if 4 * n + j > 0:
                                first_column(4 * n + j - 1)
                                take_probs(4 * n + j - 1)
                            if j == 0 and n > 0:
                                reciprocals(n - 1)
                            if j == 1 and n > 0:
                                context(n - 1)
                            if j == 2 and n > 0:
                                split_context(n - 1)
                            if j == 2 and n % 2 == 0 and n // 2 + 1 < NB:
                                rows(n // 2 + 1)
                            if j == 3 and n > 0:
                                project_out(n - 1)
                    first_column(GROUPS - 1)
                    take_probs(GROUPS - 1)
                    reciprocals(STEPS - 1)
                    context(STEPS - 1)
                    split_context(STEPS - 1)
                    project_out(STEPS - 1)

            @block.gpsimd
            def _(pool):
                P = nc.gpsimd
                def inverse_root(tiles, count):
                    pool.wait_ge(var_ready, count)
                    P.tensor_tensor(rstd[:, tiles], ve[:, tiles], power[:].to_broadcast([128, tiles.stop - tiles.start]),
                                    ALU.pow).then_inc(rstd_ready, 1)

                pool.wait_ge(w_ready, 64)
                pool.wait_ge(const_ready, 80)
                P.tensor_scalar(bias[:, 0:4], bias[:, 0:4], SCALE, None, ALU.mult).then_inc(pool_step, 2)
                pool.wait_ge(dve_step, 1)
                inverse_root(slice(CLS, CLS + 1), 1)
                inverse_root(slice(0, CLS), 2)
                pool.wait_ge(wh_ready, 2)
                P.tensor_tensor(ol[:], wo[:], oh[:].bitcast(f32), ALU.subtract).then_inc(wl_ready, 1)
                pool.sem_inc(ctx_split, 1)
                pool.sem_inc(pg_read, 2)
                pool.sem_inc(p0_done, 2)
                pool.sem_inc(pv_done, 2)
                with pool.Fori(0, ITERS) as it:
                    def rows(b):
                        for p in range(2):
                            k = it * (2 * NB) + 2 * b + p
                            pool.wait_ge(xn_ready, k + 2)
                            pool.sem_inc(pool_turn, 1)
                            h = H[:, bass.ds(k, 1), :].rearrange("q o d -> q (o d)")
                            P.tensor_tensor(h, h, bo[:], ALU.add).then_inc(hb_ready, 1)

                    def split_keys(b):
                        pool.wait_ge(qk_free, it * QK_USES + QK[("qkv", b, 5)] + 3)
                        pool.sem_inc(pool_turn, 1)
                        P.tensor_copy(qh[:, b % 2], qT[:, b % 2, :, 128:256]).then_inc(high_ready, 1)
                        P.tensor_copy(kp[:, 0], kT[:, b % 2]).then_inc(high_ready, 1)
                        pool.wait_ge(high_ready, it * (3 * NB) + 3 * b + 2)
                        pool.sem_inc(pool_turn, 1)
                        P.tensor_tensor(ql[:, b % 2], qT[:, b % 2, :, 128:256], qh[:, b % 2].bitcast(f32), ALU.subtract)
                        P.tensor_tensor(kp[:, 1], kT[:, b % 2], kp[:, 0].bitcast(f32), ALU.subtract).then_inc(high_ready, 1)
                        pool.wait_ge(high_ready, it * (3 * NB) + 3 * b + 3)
                        pool.sem_inc(pool_turn, 1)
                        for part, k_ in enumerate((kh, kl)):
                            P.tensor_tensor(k_[:, b % 2], kp[:, part].bitcast(f32).unsqueeze(1).to_broadcast([128, 4, NK + 1]),
                                            quad[:].unsqueeze(2).to_broadcast([128, 4, NK + 1]), ALU.mult).then_inc(keys_ready, 1)
                        pool.wait_ge(keys_ready, it * (2 * NB) + 2 * b + 2)

                    rows(0)
                    for b in range(NB):
                        split_keys(b)
                        if b + 1 < NB:
                            rows(b + 1)


def route_stage(nc, T, H, slot_info, slot_rows):
    f32, bf16, i32, u32 = mybir.dt.float32, mybir.dt.bfloat16, mybir.dt.int32, mybir.dt.uint32
    ALU, ACT, AX = mybir.AluOpType, mybir.ActivationFunctionType, mybir.AxisListType
    KC = DM // 128
    FC = FF // 128
    CLS = NT - 1
    GROUPS = [list(range(t, min(t + 4, NT))) for t in range(0, NT, 4)]
    TERMS = 8
    NE = NEXP

    with ExitStack() as ctx:
        sb = lambda name, shape, dt=f32: ctx.enter_context(nc.sbuf_tensor("rt_" + name, shape, dt))
        sem = lambda name: ctx.enter_context(nc.semaphore("rt_" + name))
        ident = sb("ident", [128, 128])
        upf = sb("upf", [128, 128])
        upper = sb("upper", [128, 128], bf16)
        onesb = sb("onesb", [128, 128], bf16)
        iota = sb("iota", [128, 128])
        rowid = sb("rowid", [128, 1])
        isrow = sb("isrow", [128, 1])
        rw = sb("rw", [128, KC, NE])
        eb = sb("eb", [128, NE])
        sgu = sb("sgu", [128, KC, 2 * FF])
        sdn = sb("sdn", [128, FC, DM])
        mhalf = sb("mhalf", [128, 1])
        zero = sb("zero", [128, DM + NE])
        st6 = sb("st6", [128, 6])
        mv = sb("mv", [128, 2])
        ve = sb("ve", [128, 1])
        rstd = sb("rstd", [128, 1])
        xa = sb("xa", [128, NT, DM + NE])
        xT = sb("xT", [128, KC, NT * 128])
        lT = sb("lT", [NE, 512])
        L = sb("L", [128, NT, NE])
        w = [sb(f"w{k}", [128, NT, NE]) for k in range(4)]
        score = sb("score", [128, NT, NE])
        top = sb("top", [128, NT, 8])
        topi = sb("topi", [128, NT, 8], u32)
        topf = sb("topf", [128, NT, 8])
        pick = sb("pick", [128, NT, 4, NE], bf16)
        mask = sb("mask", [128, NT, NE], bf16)
        tsum = sb("tsum", [128, NT, 1])
        cnt = sb("cnt", [128, 6, NE])
        cnti = sb("cnti", [128, NE], i32)
        prod = sb("prod", [128, 4, NE])
        pos = sb("pos", [128, NT, 4])
        posi = sb("posi", [128, 3, NT * 4], i32)
        posf = sb("posf", [128, 2, NT, 4])
        rowsel = sb("rowsel", [128, 2, 4, 128], bf16)
        slotsel = sb("slotsel", [128, 2, 4, 2, NS], bf16)
        eqs = sb("eqs", [128, 4, NS])
        info = sb("info", [128, 3, NE])
        infoc = sb("infoc", [128, 2])
        infor = sb("infor", [1, 5, 128])
        infoi = sb("infoi", [1, 128], i32)
        tabf = sb("tabf", [128, 3, NS])
        sil = sb("sil", [128, FC, 512])
        gc = sb("gc", [128, FC, 512])
        uc = sb("uc", [128, FC, 512])
        actT = sb("actT", [128, FC, 512])
        bank = [ctx.enter_context(nc.psum_tensor(f"rt_p{k}", [128, 512], f32)) for k in range(8)]
        tx, lg, lt = bank[0:2], bank[2], bank[3]
        gu = bank[0:4]
        rank = bank[4:6]
        yb = bank[4:6]
        tab, rowp = bank[6], bank[7]

        in_ready, w_ready, zero_done, x2_done, acc_done = (sem(n) for n in ("in_ready", "w_ready", "zero_done", "x2_done", "acc_done"))
        dve_step, pool_step = sem("dve_step"), sem("pool_step")
        var_ready, rstd_ready, xn_ready = sem("var_ready"), sem("rstd_ready"), sem("xn_ready")
        tx_full, tx_taken = sem("tx_full"), sem("tx_taken")
        lg_full, lg_taken, lt_full, lt_taken = sem("lg_full"), sem("lg_taken"), sem("lt_full"), sem("lt_taken")
        sp_ready, root_ready = sem("sp_ready"), sem("root_ready")
        probs_ready, mask_ready, rank_full = sem("probs_ready"), sem("mask_ready"), sem("rank_full")
        pos_ready, rowsel_ready, slotsel_ready, table_used = sem("pos_ready"), sem("rowsel_ready"), sem("slotsel_ready"), sem("table_used")
        gu_full, gu_taken, gate_ready, silu_ready, act_ready = (sem(n) for n in ("gu_full", "gu_taken", "gate_ready", "silu_ready", "act_ready"))
        y_full, y_taken, down_done = sem("y_full"), sem("y_taken"), sem("down_done")
        info_ready, row_full, rank_read = sem("info_ready"), sem("row_full"), sem("rank_read")

        with nc.Block() as block:

            @block.sync
            def _(sp):
                for dst, name in ((ident[:], "ident"), (upf[:], "upper"), (iota[:], "iota"), (rowid[:], "rowid"), (isrow[:], "isrow")):
                    sp.dma_start(dst, T[name]).then_inc(in_ready, 16)
                sp.dma_start(rw[:], T["router"]).then_inc(in_ready, 16)
                sp.dma_start(eb[:], T["ebias"].partition_broadcast(128)).then_inc(in_ready, 16)
                sp.dma_start(sgu[:], T["sgu"]).then_inc(w_ready, 16)
                sp.dma_start(sdn[:], T["sdn"]).then_inc(w_ready, 16)
                sp.wait_ge(dve_step, 1)
                sp.dma_start(T["x2"][TOKENS:TOKENS + 128, :], zero[:]).then_inc(zero_done, 16)
                sp.dma_start(T["acc"][TOKENS:TOKENS + 128, :], zero[:, 0:DM]).then_inc(zero_done, 16)
                sp.wait_ge(probs_ready, 1)
                for t in range(NT):
                    n = 128 if t < CLS else TOKENS - 128 * CLS
                    sp.dma_start(T["x2"][128 * t:128 * t + n, :], xa[0:n, t, :]).then_inc(x2_done, 16)
                for t in range(NT):
                    n = 128 if t < CLS else TOKENS - 128 * CLS
                    sp.wait_ge(y_taken, t + 1)
                    sp.dma_start(T["acc"][128 * t:128 * t + n, :], H[0:n, t, :]).then_inc(acc_done, 16)
                sp.wait_ge(zero_done, 32)
                sp.wait_ge(x2_done, 16 * NT)
                sp.wait_ge(acc_done, 16 * NT)

            @block.tensor
            def _(pe):
                M = nc.tensor.matmul
                pe.wait_ge(in_ready, 7 * 16)
                for q, tiles in enumerate(GROUPS):
                    for t in tiles:
                        pe.wait_ge(xn_ready, t + 1)
                        if t >= 2:
                            pe.wait_ge(tx_taken, t - 1)
                        for kc in range(KC):
                            last = nc.tensor.transpose(tx[t % 2][:, 128 * kc:128 * kc + 128],
                                                       xa[:, t, 128 * kc:128 * kc + 128], ident[:])
                        last.then_inc(tx_full, 1)
                    n = 128 * len(tiles)
                    pe.wait_ge(tx_taken, tiles[-1] + 1)
                    if q:
                        pe.wait_ge(lg_taken, q)
                    for kc in range(KC):
                        last = M(lg[0:NE, 0:n], rw[:, kc, :], xT[:, kc, 128 * tiles[0]:128 * tiles[0] + n],
                                 start=(kc == 0), stop=(kc == KC - 1))
                    last.then_inc(lg_full, 1)
                    pe.wait_ge(lg_taken, q + 1)
                    if q:
                        pe.wait_ge(lt_taken, q)
                    for k in range(len(tiles)):
                        last = nc.tensor.transpose(lt[:, NE * k:NE * k + NE], lT[:, 128 * k:128 * k + 128], ident[0:NE, 0:NE])
                    last.then_inc(lt_full, 1)
                pe.wait_ge(lt_taken, len(GROUPS))
                pe.wait_ge(w_ready, 32)

                def gate_up(q):
                    tiles = GROUPS[q]
                    n = 128 * len(tiles)
                    if q:
                        pe.wait_ge(gu_taken, q)
                    for m in range(2 * FC):
                        for kc in range(KC):
                            last = M(gu[m][:, 0:n], sgu[:, kc, 128 * m:128 * m + 128],
                                     xT[:, kc, 128 * tiles[0]:128 * tiles[0] + n], start=(kc == 0), stop=(kc == KC - 1))
                    last.then_inc(gu_full, 1)

                def down(q):
                    pe.wait_ge(act_ready, q + 1)
                    for k, t in enumerate(GROUPS[q]):
                        if t >= 2:
                            pe.wait_ge(y_taken, t - 1)
                        for c in range(FC):
                            last = M(yb[t % 2][:], actT[:, c, 128 * k:128 * k + 128], sdn[:, c, :],
                                     start=(c == 0), stop=(c == FC - 1))
                        last.then_inc(y_full, 1)
                    pe.wait_ge(y_full, GROUPS[q][-1] + 1)
                    pe.sem_inc(down_done, 1)

                def table(tiles):
                    for t in tiles:
                        pe.wait_ge(rowsel_ready, t + 1)
                        pe.wait_ge(slotsel_ready, t + 1)
                        for k in range(4):
                            last = M(tab[:, 0:2 * NS], rowsel[:, t % 2, k, :], slotsel[:, t % 2, k].rearrange("p a s -> p (a s)"),
                                     start=(t == 0 and k == 0), stop=(t == NT - 1 and k == 3))
                        last.then_inc(table_used, 1)

                gate_up(0)
                pe.wait_ge(mask_ready, 1)
                flat = mask[:].rearrange("p t e -> p (t e)")
                M(rank[0][:], upper[:], flat[:, 0:512], start=True, stop=False, skip_group_check=True)
                for d in range(1, NT - 1):
                    M(rank[0][:, NE * d:512], onesb[:], flat[:, 0:512 - NE * d], start=False, stop=(d == NT - 2),
                      skip_group_check=True)
                M(rank[1][:, 0:NE], upper[:], mask[:, NT - 1, :], start=True, stop=False, skip_group_check=True)
                for t in range(NT - 1):
                    M(rank[1][:, 0:NE], onesb[:], mask[:, t, :], start=False, stop=(t == NT - 2), skip_group_check=True)
                for t in range(NT):
                    last = M(rank[1][:, NE:2 * NE], onesb[:], mask[:, t, :], start=False, stop=(t == NT - 1),
                             skip_group_check=True)
                last.then_inc(rank_full, 1)
                pe.wait_ge(rank_read, 1)
                down(0)
                gate_up(1)
                down(1)
                table(range(0, 6))
                gate_up(2)
                down(2)
                table(range(6, 12))
                gate_up(3)
                down(3)
                table(range(12, NT))
                gate_up(4)
                down(4)
                pe.wait_ge(info_ready, 1)
                for k in range(2):
                    last = M(rowp[0:1, 128 * k:128 * k + 128], infoc[:, k:k + 1], ident[:], start=(k == 0), stop=True,
                             skip_group_check=True)
                last.then_inc(row_full, 1)

            @block.scalar
            def _(act):
                A = nc.scalar
                for q, tiles in enumerate(GROUPS):
                    for t in tiles:
                        act.wait_ge(tx_full, t + 1)
                        A.copy(xT[:, :, 128 * t:128 * t + 128], tx[t % 2][:].rearrange("p (k t) -> p k t", k=KC)).then_inc(tx_taken, 1)
                    act.wait_ge(lg_full, q + 1)
                    if q:
                        act.wait_ge(lt_full, q)
                    A.copy(lT[:, 0:128 * len(tiles)], lg[0:NE, 0:128 * len(tiles)]).then_inc(lg_taken, 1)
                    act.wait_ge(lt_full, q + 1)
                    A.copy(L[:, tiles[0]:tiles[-1] + 1, :].rearrange("p t e -> p (t e)"), lt[:, 0:NE * len(tiles)]).then_inc(lt_taken, 1)
                act.wait_ge(sp_ready, 1)
                A.activation(score[:].rearrange("p t e -> p (t e)"), w[2][:].rearrange("p t e -> p (t e)"), ACT.Sqrt).then_inc(root_ready, 1)
                for q, tiles in enumerate(GROUPS):
                    n = 128 * len(tiles)
                    act.wait_ge(gate_ready, q + 1)
                    A.activation(sil[:, :, 0:n], gc[:, :, 0:n], ACT.Silu).then_inc(silu_ready, 1)

            @block.vector
            def _(dve):
                V = nc.vector
                steps = [0]

                def done(ins):
                    steps[0] += 1
                    ins.then_inc(dve_step, 1)
                    dve.wait_ge(dve_step, steps[0])

                def flat(t):
                    return t[:].rearrange("p t e -> p (t e)")

                V.memset(slot_info[:], 0)
                done(V.memset(zero[:], 0.0))
                V.memset(mhalf[:], -0.5)
                done(V.memset(onesb[:], 1.0))
                dve.wait_ge(in_ready, 7 * 16)
                V.tensor_copy(upper[:], upf[:])
                for t in range(NT):
                    done(V.bn_stats(st6[:], H[:, t, :]))
                    done(V.bn_aggr(mv[:], st6[:]))
                    V.tensor_scalar(ve[:], mv[:, 1:2], 1.0, EPS, ALU.mult, ALU.add).then_inc(var_ready, 1)
                    dve.wait_ge(rstd_ready, t + 1)
                    V.tensor_scalar(xa[:, t, 0:DM], H[:, t, :], mv[:, 0:1], rstd[:], ALU.subtract, ALU.mult).then_inc(xn_ready, 1)
                    dve.wait_ge(xn_ready, t + 1)
                dve.wait_ge(lt_taken, len(GROUPS))
                e, s, s2, p = (flat(x) for x in w)
                scale = flat(w[2]).bitcast(i32)
                done(V.scalar_tensor_tensor(out=e, in0=flat(L), scalar=-1.0, in1=flat(L), op0=ALU.mult, op1=ALU.min))
                exponential(V, done, e, e, s, p, scale)
                done(V.tensor_scalar(s, e, 2.0, None, ALU.add))
                done(V.reciprocal(s2, s))
                done(V.tensor_tensor(s, e, s2, ALU.mult))
                done(V.tensor_tensor(s2, s, s, ALU.mult))
                done(V.tensor_scalar(p, s2, 1.0 / (2 * TERMS + 1), None, ALU.mult))
                for k in range(TERMS - 1, 0, -1):
                    done(V.scalar_tensor_tensor(out=p, in0=p, scalar=1.0 / (2 * k + 1), in1=s2, op0=ALU.add, op1=ALU.mult))
                done(V.scalar_tensor_tensor(out=p, in0=p, scalar=1.0, in1=s, op0=ALU.add, op1=ALU.mult))
                done(V.tensor_scalar(s, flat(L), 0.0, None, ALU.max))
                V.scalar_tensor_tensor(out=s2, in0=p, scalar=2.0, in1=s, op0=ALU.mult, op1=ALU.add).then_inc(sp_ready, 1)
                dve.wait_ge(root_ready, 1)
                done(V.tensor_scalar(s, flat(score), 1e-19, None, ALU.max))
                done(V.reciprocal(p, s))
                done(V.tensor_tensor(p, s2, p, ALU.mult))
                done(V.tensor_tensor(p, p, flat(score), ALU.add))
                done(V.tensor_scalar(flat(score), p, 0.5, None, ALU.mult))
                done(V.tensor_tensor(w[0][:], score[:], eb[:].unsqueeze(1).to_broadcast([128, NT, NE]), ALU.add))
                for t in range(NT):
                    V.max(top[:, t, :], w[0][:, t, :]).then_inc(dve_step, 1)
                steps[0] += NT
                dve.wait_ge(dve_step, steps[0])
                for t in range(NT):
                    V.max_index(topi[:, t, :], top[:, t, :], w[0][:, t, :]).then_inc(dve_step, 1)
                steps[0] += NT
                dve.wait_ge(dve_step, steps[0])
                done(V.tensor_copy(topf[:], topi[:]))
                for k in range(4):
                    V.tensor_tensor(pick[:, :, k, :], iota[:, 0:NE].unsqueeze(1).to_broadcast([128, NT, NE]),
                                    topf[:, :, k:k + 1].to_broadcast([128, NT, NE]), ALU.is_equal).then_inc(dve_step, 1)
                steps[0] += 4
                dve.wait_ge(dve_step, steps[0])
                cls_pick = pick[:, CLS].rearrange("p k e -> p (k e)")
                done(V.tensor_scalar(cls_pick, cls_pick, isrow[:], None, ALU.mult))
                V.tensor_tensor(w[1][:], pick[:, :, 0, :], pick[:, :, 1, :], ALU.add)
                done(V.tensor_tensor(w[2][:], pick[:, :, 2, :], pick[:, :, 3, :], ALU.add))
                done(V.tensor_tensor(w[3][:], w[1][:], w[2][:], ALU.add))
                V.tensor_copy(mask[:], w[3][:]).then_inc(mask_ready, 1)
                done(V.tensor_tensor(w[1][:], w[3][:], score[:], ALU.mult))
                done(V.tensor_reduce(out=tsum[:].rearrange("p t o -> p (t o)"), in_=w[1][:], axis=AX.X, op=ALU.add))
                done(V.tensor_scalar(tsum[:], tsum[:], 1e-20, None, ALU.add))
                done(V.reciprocal(tsum[:], tsum[:]))
                V.tensor_tensor(xa[:, :, DM:], w[1][:], tsum[:].to_broadcast([128, NT, NE]), ALU.mult).then_inc(probs_ready, 1)

                def clipped(q):
                    n = 128 * len(GROUPS[q])
                    dve.wait_ge(gu_full, q + 1)
                    if q:
                        dve.wait_ge(silu_ready, q)
                    for c in range(FC):
                        last = V.tensor_scalar(gc[:, c, 0:n], gu[c][:, 0:n], -ALPHA, ALPHA, ALU.max, ALU.min)
                    last.then_inc(gate_ready, 1)
                    for c in range(FC):
                        last = V.tensor_scalar(uc[:, c, 0:n], gu[FC + c][:, 0:n], -ALPHA, ALPHA, ALU.max, ALU.min)
                    last.then_inc(gu_taken, 1)
                    dve.wait_ge(gu_taken, q + 1)
                    dve.wait_ge(silu_ready, q + 1)
                    if q:
                        dve.wait_ge(down_done, q)
                    V.tensor_tensor(actT[:, :, 0:n], sil[:, :, 0:n], uc[:, :, 0:n], ALU.mult).then_inc(act_ready, 1)

                def add_shared(q):
                    for t in GROUPS[q]:
                        dve.wait_ge(y_full, t + 1)
                        V.tensor_tensor(H[:, t, :], H[:, t, :], yb[t % 2][:], ALU.add).then_inc(y_taken, 1)

                def select_slots(tiles):
                    for t in tiles:
                        if t >= 2:
                            dve.wait_ge(table_used, t - 1)
                        done(V.tensor_tensor(eqs[:], iota[:, 0:NS].unsqueeze(1).to_broadcast([128, 4, NS]),
                                             posf[:, 0, t, :].unsqueeze(2).to_broadcast([128, 4, NS]), ALU.is_equal))
                        done(V.tensor_scalar(slotsel[:, t % 2, :, 0, :], eqs[:], rowid[:], None, ALU.mult))
                        V.tensor_scalar(slotsel[:, t % 2, :, 1, :], eqs[:], float(t + 1), None, ALU.mult).then_inc(slotsel_ready, 1)
                        dve.wait_ge(slotsel_ready, t + 1)

                clipped(0)
                dve.wait_ge(rank_full, 1)
                n_, tiles_, end_, tmp_ = cnt[:, 0, :], cnt[:, 1, :], cnt[:, 2, :], cnt[:, 3, :]
                done(V.tensor_copy(n_, rank[1][:, NE:2 * NE]))
                done(V.tensor_scalar(cnti[:], n_, 127.0, None, ALU.add))
                done(V.tensor_scalar(cnti[:], cnti[:], 7, None, ALU.logical_shift_right))
                done(V.tensor_copy(tiles_, cnti[:]))
                src, dst = tiles_, end_
                for k in range(5):
                    d = 1 << k
                    V.tensor_copy(dst[:, 0:d], src[:, 0:d])
                    done(V.tensor_tensor(dst[:, d:], src[:, d:], src[:, :NE - d], ALU.add))
                    src, dst = dst, (tmp_ if dst is end_ else end_)
                end_ = src
                done(V.tensor_tensor(cnt[:, 4, :], end_, tiles_, ALU.subtract))
                done(V.tensor_scalar(cnt[:, 4, :], cnt[:, 4, :], 128.0, None, ALU.mult))
                V.tensor_tensor(w[0][:, 0:NT - 1, :], rank[0][:].rearrange("p (t e) -> p t e", e=NE),
                                cnt[:, 4, :].unsqueeze(1).to_broadcast([128, NT - 1, NE]), ALU.add)
                V.tensor_tensor(w[0][:, NT - 1, :], rank[1][:, 0:NE], cnt[:, 4, :], ALU.add).then_inc(rank_read, 1)
                dve.wait_ge(rank_read, 1)
                for k in range(4):
                    done(V.tensor_tensor(w[1][:], w[0][:], pick[:, :, k, :], ALU.mult))
                    done(V.tensor_reduce(out=pos[:, :, k:k + 1].rearrange("p t o -> p (t o)"), in_=w[1][:], axis=AX.X, op=ALU.add))
                pi = lambda k: posi[:, k, :]
                done(V.tensor_copy(pi(0), pos[:].rearrange("p t k -> p (t k)")))
                V.tensor_scalar(pi(1), pi(0), 7, None, ALU.logical_shift_right)
                done(V.tensor_scalar(pi(2), pi(0), 127, None, ALU.bitwise_and))
                V.tensor_copy(posf[:, 0].rearrange("p t k -> p (t k)"), pi(1))
                done(V.tensor_copy(posf[:, 1].rearrange("p t k -> p (t k)"), pi(2)))
                V.tensor_scalar(posf[:, 0, CLS, :], posf[:, 0, CLS, :], 1.0, isrow[:], ALU.add, ALU.mult).then_inc(dve_step, 1)
                steps[0] += 1
                dve.wait_ge(dve_step, steps[0])
                V.tensor_scalar(posf[:, 0, CLS, :], posf[:, 0, CLS, :], -1.0, None, ALU.add).then_inc(pos_ready, 1)
                dve.wait_ge(pos_ready, 1)
                V.tensor_scalar(info[:, 0, :], end_, rowid[:], None, ALU.is_le)
                done(V.tensor_scalar(info[:, 1, :], tiles_, 0.0, None, ALU.is_gt))
                done(V.tensor_tensor(info[:, 2, :], info[:, 0, :], info[:, 1, :], ALU.mult))
                V.tensor_reduce(out=infoc[:, 0:1], in_=info[:, 0, :], axis=AX.X, op=ALU.add)
                V.tensor_reduce(out=infoc[:, 1:2], in_=info[:, 2, :], axis=AX.X, op=ALU.add).then_inc(info_ready, 1)
                add_shared(0)
                clipped(1)
                add_shared(1)
                select_slots(range(0, 6))
                clipped(2)
                add_shared(2)
                select_slots(range(6, 12))
                clipped(3)
                add_shared(3)
                select_slots(range(12, NT))
                dve.wait_ge(table_used, NT)
                V.tensor_scalar(tabf[:, 0, :], tab[:, NS:2 * NS], 0.0, None, ALU.is_equal)
                done(V.tensor_scalar(tabf[:, 1, :], tab[:, NS:2 * NS], 128.0, -128.0, ALU.mult, ALU.add))
                done(V.tensor_tensor(tabf[:, 1, :], tabf[:, 1, :], tab[:, 0:NS], ALU.add))
                V.tensor_scalar(ve[:], rowid[:], float(TOKENS + 128), None, ALU.add).then_inc(dve_step, 1)
                steps[0] += 1
                dve.wait_ge(dve_step, steps[0])
                done(V.scalar_tensor_tensor(out=tabf[:, 2, :], in0=tabf[:, 0, :], scalar=ve[:], in1=tabf[:, 1, :],
                                            op0=ALU.mult, op1=ALU.add))
                done(V.tensor_copy(slot_rows[:], tabf[:, 2, :]))
                clipped(4)
                add_shared(4)
                dve.wait_ge(row_full, 1)
                V.tensor_scalar(infor[:, 0, :], rowp[0:1, 0:128], float(NE - 1), None, ALU.min)
                done(V.tensor_scalar(infor[:, 3, :], rowp[0:1, 0:128], float(NE), None, ALU.is_lt))
                V.tensor_reduce(out=infor[:, 4, 0:1], in_=infor[:, 3, :].rearrange("o (g f) -> o g f", f=UN)[:, :, 0],
                                axis=AX.X, op=ALU.add)
                done(V.tensor_copy(infor[:, 1, :], rowp[0:1, 128:256]))
                V.memset(infor[:, 2, 0:1], 1.0)
                V.tensor_tensor(infor[:, 2, 1:128], infor[:, 1, 1:128], infor[:, 1, 0:127], ALU.not_equal)
                done(V.tensor_copy(infoi[:], infor[:, 1, :]))
                done(V.tensor_scalar(infoi[:], infoi[:], WBUF - 1, None, ALU.bitwise_and))
                si = slot_info[:].rearrange("o (s f) -> o s f", f=4)
                V.tensor_copy(si[:, :, 0], infor[:, 0, :])
                V.tensor_copy(si[:, :, 1], infor[:, 2, :])
                V.tensor_copy(si[:, :, 2], infoi[:])
                done(V.tensor_copy(si[:, :, 3], infor[:, 3, :]))
                V.tensor_copy(si[:, 127, 3:4], infor[:, 4, 0:1])

            @block.gpsimd
            def _(pool):
                P = nc.gpsimd
                pool.wait_ge(dve_step, 2)
                for t in range(NT):
                    pool.wait_ge(var_ready, t + 1)
                    P.tensor_tensor(rstd[:], ve[:], mhalf[:], ALU.pow).then_inc(rstd_ready, 1)
                pool.wait_ge(pos_ready, 1)
                for t in range(NT):
                    if t >= 2:
                        pool.wait_ge(table_used, t - 1)
                    for k in range(4):
                        last = P.tensor_scalar(rowsel[:, t % 2, k, :], iota[:], posf[:, 1, t, k:k + 1], None, ALU.is_equal)
                    last.then_inc(rowsel_ready, 1)


def expert_stage(nc, T, slot_info, slot_rows):
    f32, i32 = mybir.dt.float32, mybir.dt.uint32
    ALU, ACT = mybir.AluOpType, mybir.ActivationFunctionType
    KC = DM // 128
    FC = FF // 128
    ITERS = SLOTS // UN
    WCOLS = KC * 2 * FF + FC * DM
    assert UN == WBUF and SLOTS % UN == 0

    with ExitStack() as ctx:
        sb = lambda name, shape, dt=f32: ctx.enter_context(nc.sbuf_tensor("ex_" + name, shape, dt))
        sem = lambda name: ctx.enter_context(nc.semaphore("ex_" + name))
        ident = sb("ident", [128, 128])
        wt = sb("wt", [128, WBUF * WCOLS])
        gidx = [sb(f"gidx{n}", [128, 1], i32) for n in range(4)]
        sidx = [sb(f"sidx{n}", [128, 1], i32) for n in range(2)]
        xg = [sb(f"xg{n}", [128, DM + NEXP]) for n in range(4)]
        share = sb("share", [128, 4])
        xT = [sb(f"xT{n}", [128, KC, 128]) for n in range(2)]
        gc = sb("gc", [128, FF])
        uc = sb("uc", [128, FF])
        sil = sb("sil", [128, FF])
        act_ = sb("act", [128, FF])
        actT = sb("actT", [128, FC, 128])
        ys = [sb(f"ys{n}", [128, DM]) for n in range(2)]
        pb = lambda name: ctx.enter_context(nc.psum_tensor("ex_" + name, [128, 512], f32))
        tx, ta = pb("tx"), pb("ta")
        gu = [pb(f"gu{n}") for n in range(2)]
        yb = [pb(f"y{n}") for n in range(2)]
        ident_ready = sem("ident_ready")
        w_ready = [sem(f"w_ready{n}") for n in range(2)]
        gathered = [sem(f"gathered{n}") for n in range(4)]
        scattered = [sem(f"scattered{n}") for n in range(2)]
        idx_ready, share_ready, sidx_ready, sent = (sem(n) for n in ("idx_ready", "share_ready", "sidx_ready", "sent"))
        tx_full, tx_taken = sem("tx_full"), sem("tx_taken")
        ta_full, ta_taken = sem("ta_full"), sem("ta_taken")
        gu_full, gate_ready, gu_taken, silu_ready, act_ready = (sem(n) for n in ("gu_full", "gate_ready", "gu_taken", "silu_ready", "act_ready"))
        y_full, y_ready = sem("y_full"), sem("y_ready")
        pe_turn, pool_turn, sp_turn = (sem(n) for n in ("pe_turn", "pool_turn", "sp_turn"))

        W_SEED, TX_SEED, GU_SEED, TA_SEED, Y_SEED, SENT_SEED = 4, 2, 1, 1, 2, 2

        def used(engine, it):
            return engine.If(engine.value_load(slot_info[0:1, bass.ds(it * (4 * UN) + 3, 1)], min_val=0, max_val=1))

        def turns(engine):
            return engine.value_load(slot_info[0:1, 4 * 127 + 3:4 * 128], min_val=1, max_val=ITERS)

        with nc.Block() as block:

            @block.sync
            def _(sp):
                sp.dma_start(ident[:], T["ident"]).then_inc(ident_ready, 16)

                def load(slot, n):
                    expert = sp.value_load(slot_info[0:1, bass.ds(slot * 4, 1)], min_val=0, max_val=NEXP - 1)
                    first = sp.value_load(slot_info[0:1, bass.ds(slot * 4 + 1, 1)], min_val=0, max_val=1)
                    buf = sp.value_load(slot_info[0:1, bass.ds(slot * 4 + 2, 1)], min_val=0, max_val=WBUF - 1)
                    sp.dma_start(wt[:, bass.ds(buf * WCOLS, WCOLS)],
                                 T["wexp"][bass.ds(expert, 1), :, :].rearrange("o p n -> p (o n)"),
                                 cond=first).then_inc(w_ready[n % 2], 16)

                load(0, 0)
                sp.sem_inc(y_full, W_SEED)
                with sp.Fori(0, ITERS) as it:
                    with used(sp, it):
                        for n in range(UN):
                            sp.wait_ge(y_full, it * UN + n - 2 + W_SEED)
                            sp.sem_inc(sp_turn, 1)
                            load(it * UN + n + 1, n + 1)
                            sp.wait_ge(w_ready[n % 2], (it * (UN // 2) + n // 2) * 16 + 16)
                            sp.sem_inc(sp_turn, 1)
                sp.wait_ge(w_ready[0], turns(sp) * (16 * UN // 2) + 16)
                sp.sem_inc(sp_turn, 1)

            @block.tensor
            def _(pe):
                M = nc.tensor.matmul

                def transpose_rows(n, count):
                    pe.wait_ge(tx_taken, count)
                    pe.sem_inc(pe_turn, 1)
                    for kc in range(KC):
                        last = nc.tensor.transpose(tx[:, 128 * kc:128 * kc + 128], xg[n % 4][:, 128 * kc:128 * kc + 128], ident[:])
                    last.then_inc(tx_full, 1)

                def weights(slot):
                    buf = pe.value_load(slot_info[0:1, bass.ds(slot * 4 + 2, 1)], min_val=0, max_val=WBUF - 1)
                    return pe.snap(buf * WCOLS)

                def gate_up(n, base, chunks):
                    for kc in chunks:
                        last = M(gu[n % 2][:], xT[n % 2][:, kc, :], wt[:, bass.ds(base + kc * 2 * FF, 2 * FF)],
                                 start=(kc == 0), stop=(kc == KC - 1))
                    if kc == KC - 1:
                        last.then_inc(gu_full, 1)

                pe.wait_ge(ident_ready, 16)
                pe.wait_ge(gathered[0], 16)
                transpose_rows(0, 2)
                pe.wait_ge(tx_taken, 3)
                pe.wait_ge(w_ready[0], 16)
                base = weights(0)
                gate_up(0, base, range(KC))
                pe.wait_ge(gathered[1], 16)
                transpose_rows(1, 3)
                with pe.Fori(0, ITERS) as it:
                    with used(pe, it):
                        base = weights(it * UN)
                        for n in range(UN):
                            s = it * UN + n
                            pe.wait_ge(gathered[(n + 2) % 4], (it + (n + 2) // 4) * 16 + 16)
                            transpose_rows(n + 2, s + 4)
                            pe.wait_ge(w_ready[(n + 1) % 2], (it * (UN // 2) + (n + 1) // 2) * 16 + 16)
                            pe.wait_ge(gu_taken, s + 1)
                            nxt = weights(s + 1)
                            gate_up(n + 1, nxt, range(KC // 2))
                            pe.wait_ge(act_ready, s + 1)
                            pe.wait_ge(ta_taken, s + 1)
                            pe.sem_inc(pe_turn, 1)
                            for c in range(FC):
                                last = nc.tensor.transpose(ta[:, 128 * c:128 * c + 128], act_[:, 128 * c:128 * c + 128], ident[:])
                            last.then_inc(ta_full, 1)
                            gate_up(n + 1, nxt, range(KC // 2, KC))
                            pe.wait_ge(ta_taken, s + 2)
                            pe.wait_ge(y_ready, s + 1)
                            for c in range(FC):
                                last = M(yb[n % 2][:], actT[:, c, :], wt[:, bass.ds(base + KC * 2 * FF + c * DM, DM)],
                                         start=(c == 0), stop=(c == FC - 1))
                            last.then_inc(y_full, 1)
                            base = nxt

            @block.scalar
            def _(act):
                A = nc.scalar
                act.sem_inc(ta_taken, TA_SEED)
                act.sem_inc(y_ready, Y_SEED)
                act.sem_inc(sent, SENT_SEED)
                with act.Fori(0, ITERS) as it:
                    with used(act, it):
                        for n in range(UN):
                            s = it * UN + n
                            act.wait_ge(gate_ready, s + 1)
                            A.activation(sil[:], gc[:], ACT.Silu).then_inc(silu_ready, 1)
                            act.wait_ge(ta_full, s + 1)
                            A.copy(actT[:].rearrange("p c t -> p (c t)"), ta[:, 0:FF]).then_inc(ta_taken, 1)
                            act.wait_ge(y_full, s + 1 + W_SEED)
                            act.wait_ge(sent, s + 1)
                            act.wait_ge(share_ready, s + 1)
                            A.activation(ys[n % 2][:], yb[n % 2][:], ACT.Copy, scale=share[:, n:n + 1]).then_inc(y_ready, 1)

            @block.vector
            def _(dve):
                V = nc.vector

                def take_rows(n, count):
                    dve.wait_ge(tx_full, count)
                    V.tensor_copy(xT[n % 2][:].rearrange("p k t -> p (k t)"), tx[:]).then_inc(tx_taken, 1)

                dve.sem_inc(tx_taken, TX_SEED)
                dve.sem_inc(gu_taken, GU_SEED)
                take_rows(0, 1)
                take_rows(1, 2)
                with dve.Fori(0, ITERS) as it:
                    with used(dve, it):
                        for n in range(UN):
                            s = it * UN + n
                            dve.wait_ge(gu_full, s + 1)
                            V.tensor_scalar(gc[:], gu[n % 2][:, 0:FF], -ALPHA, ALPHA, ALU.max, ALU.min).then_inc(gate_ready, 1)
                            V.tensor_scalar(uc[:], gu[n % 2][:, FF:2 * FF], -ALPHA, ALPHA, ALU.max, ALU.min).then_inc(gu_taken, 1)
                            dve.wait_ge(gu_taken, s + 2)
                            dve.wait_ge(silu_ready, s + 1)
                            V.tensor_tensor(act_[:], sil[:], uc[:], ALU.mult).then_inc(act_ready, 1)
                            take_rows(n + 2, s + 3)

            @block.gpsimd
            def _(pool):
                P = nc.gpsimd

                def gather(slot, n, count):
                    P.tensor_copy(gidx[n % 4][:], slot_rows[:, bass.ds(slot, 1)]).then_inc(idx_ready, 1)
                    pool.wait_ge(idx_ready, count + 1)
                    pool.sem_inc(pool_turn, 1)
                    P.indirect_dma_start(xg[n % 4][:], None, T["x2"], bass.IndirectOffsetOnAxis(ap=gidx[n % 4][:], axis=0)
                                         ).then_inc(gathered[n % 4], 16)

                def take_share(slot, n):
                    expert = pool.value_load(slot_info[0:1, bass.ds(slot * 4, 1)], min_val=0, max_val=NEXP - 1)
                    P.tensor_copy(share[:, n % 4:n % 4 + 1], xg[n % 4][:, bass.ds(expert + DM, 1)]).then_inc(share_ready, 1)

                def take_rows_index(slot, n):
                    P.tensor_copy(sidx[n % 2][:], slot_rows[:, bass.ds(slot, 1)]).then_inc(sidx_ready, 1)

                for n in range(4):
                    gather(n, n, n)
                for n in range(2):
                    pool.wait_ge(gathered[n], 16)
                    take_share(n, n)
                pool.wait_ge(tx_taken, 1 + TX_SEED)
                pool.wait_ge(share_ready, 1)
                gather(4, 0, 4)
                take_rows_index(0, 0)
                with pool.Fori(0, ITERS) as it:
                    with used(pool, it):
                        for n in range(UN):
                            s = it * UN + n
                            pool.wait_ge(sidx_ready, s + 1)
                            pool.wait_ge(y_ready, s + 1 + Y_SEED)
                            pool.sem_inc(pool_turn, 1)
                            P.indirect_dma_start(T["acc"], bass.IndirectOffsetOnAxis(ap=sidx[n % 2][:], axis=0), ys[n % 2][:],
                                                 None, compute_op=ALU.add).then_inc(scattered[n % 2], 16)
                            pool.wait_ge(tx_taken, s + 2 + TX_SEED)
                            pool.wait_ge(share_ready, s + 2)
                            pool.sem_inc(pool_turn, 1)
                            gather(s + 5, n + 1, s + 5)
                            pool.wait_ge(gathered[(n + 2) % 4], (it + (n + 2) // 4) * 16 + 16)
                            pool.sem_inc(pool_turn, 1)
                            take_share(s + 2, n + 2)
                            take_rows_index(s + 1, n + 1)
                            pool.wait_ge(scattered[n % 2], (it * (UN // 2) + n // 2) * 16 + 16)
                            pool.sem_inc(sent, 1)
                last = turns(pool)
                for n in range(4):
                    pool.wait_ge(gathered[n], last * 16 + (32 if n == 0 else 16))
                    pool.sem_inc(pool_turn, 1)


def output_stage(nc, T):
    with nc.semaphore("out_done") as out_done, nc.Block() as block:

        @block.sync
        def _(sp):
            for c in range(NCH):
                sp.dma_start(T["out"][c, 1:, :], T["acc"][256 * c:256 * c + 256, :]).then_inc(out_done, 16)
            sp.dma_start(T["out"][:, 0, :], T["acc"][256 * NCH:256 * NCH + NCH, :]).then_inc(out_done, 16)
            sp.wait_ge(out_done, 16 * (NCH + 1))


def build(nc, T):
    f32, u32, i32 = mybir.dt.float32, mybir.dt.uint32, mybir.dt.int32
    T["hs"] = nc.dram_tensor("ssm_rows", (128, 128, 64), f32).ap()
    T["x2"] = nc.dram_tensor("x2_rows", (TOKENS + 128, DM + NEXP), f32).ap()
    T["acc"] = nc.dram_tensor("acc_rows", (TOKENS + 128, DM), f32).ap()
    with ExitStack() as ctx:
        slot_info = ctx.enter_context(nc.sbuf_tensor("slot_info", [1, 4 * 128], i32))
        slot_rows = ctx.enter_context(nc.sbuf_tensor("slot_rows", [128, NS], u32))
        ssm_stage(nc, T)
        with nc.sbuf_tensor("H", [128, NT, DM], f32) as H:
            attention_stage(nc, T, H)
            route_stage(nc, T, H, slot_info, slot_rows)
        expert_stage(nc, T, slot_info, slot_rows)
        output_stage(nc, T)


def laid_out(x, cls_tok, L0_tok_log_dt, L0_tok_B_ri, L0_tok_inv_A_real, L0_tok_A_imag, L0_attn_c_attn_w, L0_attn_c_attn_b,
             L0_attn_c_proj_w, L0_attn_c_proj_b, L0_ffn_router_w, L0_ffn_expert_bias, L0_ffn_gate_w, L0_ffn_up_w,
             L0_ffn_down_w, L0_ffn_shared_gate_w, L0_ffn_shared_up_w, L0_ffn_shared_down_w):
    def chunks(a):
        return a.reshape(a.shape[0] // 128, 128, a.shape[1]).transpose(1, 0, 2)

    par = np.stack([L0_tok_inv_A_real, L0_tok_A_imag, L0_tok_B_ri[..., 0], L0_tok_B_ri[..., 1]])
    wt, b = chunks(L0_attn_c_attn_w.T), L0_attn_c_attn_b
    k, v = slice(DM, DM + HD), slice(DM + HD, DM + 2 * HD)
    selh = np.zeros((128, 4, 128), np.float32)
    for j in range(4):
        for m in range(4):
            selh[4 * j + m, m, 32 * j:32 * j + 32] = 1.0
    gu = np.concatenate([L0_ffn_gate_w, L0_ffn_up_w], axis=1)
    gu = gu.reshape(NEXP, 2 * FF, DM // 128, 128).transpose(0, 3, 2, 1).reshape(NEXP, 128, -1)
    dn = L0_ffn_down_w.reshape(NEXP, DM, FF // 128, 128).transpose(0, 3, 2, 1).reshape(NEXP, 128, -1)
    row, col = np.arange(128)[:, None], np.arange(128)[None, :]
    return {
        "ssm_par": par.reshape(4, 2, 128, 64).transpose(1, 3, 0, 2).reshape(128, 4, 128),
        "log_dt": L0_tok_log_dt.reshape(2, 128),
        "c_ri": x.reshape(NCH, 2, 128, 64, 2).transpose(1, 3, 4, 2, 0).reshape(128, 2, 128 * NCH),
        "watt": np.concatenate([wt[:, :, 0:DM]] + [wt[:, :, k]] * 4 + [wt[:, :, v]] * 4, axis=2),
        "battn": np.concatenate([b[:DM].reshape(4, 128).T, np.tile(b[k], 4)[:, None], np.tile(b[v], 4)[:, None]], axis=1),
        "wo": chunks(L0_attn_c_proj_w.T),
        "bo": L0_attn_c_proj_b.reshape(1, DM),
        "cls": cls_tok.reshape(1, DM),
        "selh": selh,
        "quad": (row // 32 == np.arange(4)).astype(np.float32),
        "selv": np.roll(selh, 32, axis=0),
        "mask": np.where(col <= row, 0.0, -3e38).astype(np.float32),
        "ident": np.eye(128, dtype=np.float32),
        "upper": (row < col).astype(np.float32),
        "iota": np.broadcast_to(col, (128, 128)).astype(np.float32),
        "rowid": row.astype(np.float32),
        "isrow": (row < NCH).astype(np.float32),
        "router": chunks(L0_ffn_router_w.T),
        "ebias": L0_ffn_expert_bias.reshape(1, NEXP),
        "sgu": chunks(np.concatenate([L0_ffn_shared_gate_w, L0_ffn_shared_up_w], axis=0).T),
        "sdn": chunks(L0_ffn_shared_down_w.T),
        "wexp": np.concatenate([gu, dn], axis=2),
    }


def kernel(**inputs):
    import concourse.bacc as bacc
    from concourse.bass_utils import run_bass_kernel_spmd

    arrays = {f"in_{n}_dram": np.ascontiguousarray(a) for n, a in laid_out(**{n: np.asarray(a) for n, a in inputs.items()}).items()}
    nc = bacc.Bacc("TRN2", target_bir_lowering=False, num_devices=1)
    T = {n[3:-5]: nc.dram_tensor(n, a.shape, mybir.dt.from_np(a.dtype), kind="ExternalInput").ap() for n, a in arrays.items()}
    T["out"] = nc.dram_tensor("out_dram", (NCH, 1 + 256, DM), mybir.dt.float32, kind="ExternalOutput").ap()
    build(nc, T)
    r = run_bass_kernel_spmd(nc, [arrays], core_ids=[0])
    return r.results[0]["out_dram"]
```

```python
from contextlib import ExitStack

import numpy as np

import concourse.bass as bass
from concourse import mybir

NCH = 8
SEQ = 512
DM = 512
HD = 32
EPS = 1e-5
NEXP = 32
FF = 256
ALPHA = 7.0
NT = 17
TOKENS = 128 * (NT - 1) + NCH
SLOTS = TOKENS * 4 // 128 + NEXP
NS = SLOTS + 5
WBUF = 4
UN = 4




def exponential(V, done, out, x, t, k, scale):
    ALU = mybir.AluOpType
    ROUND = 1.5 * 2.0 ** 23
    LN2_HI = 0.693359375
    LN2_LO = float(np.log(2.0)) - LN2_HI
    done(V.tensor_scalar(t, x, -88.0, 89.0, ALU.max, ALU.min))
    done(V.tensor_scalar(k, t, float(1 / np.log(2.0)), ROUND, ALU.mult, ALU.add))
    done(V.tensor_scalar(k, k, ROUND, None, ALU.subtract))
    done(V.scalar_tensor_tensor(out=t, in0=k, scalar=-LN2_HI, in1=t, op0=ALU.mult, op1=ALU.add))
    done(V.scalar_tensor_tensor(out=t, in0=k, scalar=-LN2_LO, in1=t, op0=ALU.mult, op1=ALU.add))
    done(V.tensor_scalar(scale, k, 127.0, None, ALU.add))
    done(V.tensor_scalar(scale, scale, 23, None, ALU.logical_shift_left))
    fact = [1.0]
    for n in range(1, 8):
        fact.append(fact[-1] * n)
    done(V.tensor_scalar(k, t, 1 / fact[7], None, ALU.mult))
    for n in range(6, 0, -1):
        done(V.scalar_tensor_tensor(out=k, in0=k, scalar=1 / fact[n], in1=t, op0=ALU.add, op1=ALU.mult))
    done(V.scalar_tensor_tensor(out=out, in0=k, scalar=1.0, in1=scale.bitcast(mybir.dt.float32), op0=ALU.add, op1=ALU.mult))
def ssm_stage(nc, T, preload):
    f32 = mybir.dt.float32
    ALU = mybir.AluOpType
    ACT = mybir.ActivationFunctionType
    NI = 128
    IC = 16
    CHUNKS = NI // IC
    LB = 64
    LA = SEQ // LB
    AC = LA * NCH
    PW = 9
    with ExitStack() as ctx:
        sb = lambda name, shape, dt=f32: ctx.enter_context(nc.sbuf_tensor(name, shape, dt))
        sem = lambda name: ctx.enter_context(nc.semaphore(name))
        par = sb("ssm_par", [128, 5, NI])
        cri = sb("ssm_c", [128, 2, NI * NCH])
        ex = sb("ssm_exp", [128, 2, NI])
        exi = sb("ssm_exp_scale", [128, 2, NI], mybir.dt.int32)
        wk = sb("ssm_work", [128, 10, NI])
        ng = sb("ssm_minus_g", [128, 2, NI])
        z = sb("ssm_z", [128, PW, 2, NI])
        vb = [sb(f"ssm_v{n}", [128, 2, IC, LB]) for n in range(2)]
        qb = [sb(f"ssm_q{n}", [128, 2, IC, AC]) for n in range(2)]
        tv = sb("ssm_tv", [128, 2, 2, IC, LB // 2])
        tq = sb("ssm_tq", [128, 2, 2, IC, AC // 2])
        tc = sb("ssm_tc", [128, 2, 2, IC, NCH])
        kb = [sb(f"ssm_k{n}", [128, IC, LB]) for n in range(2)]
        ps = [ctx.enter_context(nc.psum_tensor(f"ssm_ps{n}", [128, IC, LB], f32)) for n in range(2)]
        in_ready = sem("ssm_in_ready")
        preloaded = sem("ssm_preloaded")
        dve_step = sem("ssm_dve_step")
        pool_step = sem("ssm_pool_step")
        v_free = [sem(f"ssm_v_free{n}") for n in range(2)]
        q_free = [sem(f"ssm_q_free{n}") for n in range(2)]
        ps_free = [sem(f"ssm_ps_free{n}") for n in range(2)]
        prod_ready = sem("ssm_prod_ready")
        turn = sem("ssm_turn")
        k_ready = sem("ssm_k_ready")
        k_free = [sem(f"ssm_k_free{n}") for n in range(2)]
        k_stored = [sem(f"ssm_k_stored{n}") for n in range(2)]
        z_steps = []
        block = ctx.enter_context(nc.Block())

        @block.sync
        def _(sp):
            sp.dma_start(par[:, 1:, :], T["ssm_par"]).then_inc(in_ready, 16)
            for p in range(2):
                sp.dma_start(par[64 * p:64 * p + 64, 0, :],
                             T["log_dt"][p:p + 1, :].partition_broadcast(64)).then_inc(in_ready, 16)
            sp.dma_start(cri[:], T["c_ri"]).then_inc(in_ready, 16)
            for tile, source in preload:
                sp.dma_start(tile, source).then_inc(preloaded, 16)
            with sp.Fori(0, CHUNKS // 2) as it:
                for n in range(2):
                    sp.wait_ge(k_ready, it * 2 + n + 1)
                    sp.dma_start(T["hs"][:, bass.ds(it * (2 * IC) + n * IC, IC), :], kb[n][:]).then_inc(k_stored[n], 16)
                    sp.wait_ge(k_stored[n], it * 16 + 16)
                    sp.sem_inc(k_free[n], 1)
            sp.wait_ge(preloaded, 16 * len(preload))

        @block.scalar
        def _(act):
            for n in range(2):
                act.sem_inc(k_free[n], 1)
                act.sem_inc(ps_free[n], 1)
            with act.Fori(0, CHUNKS // 2) as it:
                for n in range(2):
                    act.wait_ge(prod_ready, it * 2 + n + 1)
                    act.wait_ge(k_free[n], it + 1)
                    nc.scalar.copy(kb[n][:], ps[n][:]).then_inc(k_ready, 1)
                    act.wait_ge(k_ready, it * 2 + n + 1)
                    act.sem_inc(ps_free[n], 1)

        @block.vector
        def _(dve):
            V = nc.vector
            steps = [0]

            def done(ins):
                steps[0] += 1
                ins.then_inc(dve_step, 1)
                dve.wait_ge(dve_step, steps[0])

            w = lambda k: wk[:, k, :]
            dve.wait_ge(in_ready, 64)
            exponential(V, done, ex[:], par[:, 0:2, :], wk[:, 0:2, :], wk[:, 2:4, :], exi[:])
            dt_, dec = ex[:, 0, :], ex[:, 1, :]
            V.scalar_tensor_tensor(out=w(0), in0=dec, scalar=-0.5, in1=dt_, op0=ALU.mult, op1=ALU.mult)
            done(V.scalar_tensor_tensor(out=w(1), in0=par[:, 2, :], scalar=0.5, in1=dt_, op0=ALU.mult, op1=ALU.mult))
            V.tensor_scalar(w(2), w(0), -1.0, 1.0, ALU.mult, ALU.add)
            V.tensor_tensor(w(3), w(0), w(0), ALU.mult)
            done(V.tensor_tensor(w(4), w(1), w(1), ALU.mult))
            V.tensor_tensor(w(5), w(2), w(2), ALU.mult)
            done(V.tensor_tensor(w(6), w(3), w(4), ALU.add))
            done(V.tensor_tensor(w(5), w(5), w(4), ALU.add))
            done(V.reciprocal(w(7), w(5)))
            V.tensor_scalar(w(6), w(6), -1.0, 1.0, ALU.mult, ALU.add)
            V.scalar_tensor_tensor(out=z[:, 0, 1, :], in0=w(1), scalar=2.0, in1=w(7), op0=ALU.mult, op1=ALU.mult)
            done(V.scalar_tensor_tensor(out=w(8), in0=w(7), scalar=-2.0, in1=dt_, op0=ALU.mult, op1=ALU.mult))
            V.tensor_tensor(z[:, 0, 0, :], w(6), w(7), ALU.mult)
            V.tensor_tensor(w(2), w(2), w(8), ALU.mult)
            done(V.tensor_tensor(w(1), w(1), w(8), ALU.mult))
            V.tensor_tensor(w(3), par[:, 3, :], w(2), ALU.mult)
            V.tensor_tensor(w(4), par[:, 4, :], w(1), ALU.mult)
            V.tensor_tensor(w(5), par[:, 3, :], w(1), ALU.mult)
            done(V.tensor_tensor(w(6), par[:, 4, :], w(2), ALU.mult))
            V.tensor_tensor(ng[:, 0, :], w(3), w(4), ALU.subtract)
            done(V.tensor_tensor(ng[:, 1, :], w(5), w(6), ALU.add))
            for k in range(PW - 1):
                V.tensor_tensor(w(0), z[:, k, 0, :], z[:, k, 0, :], ALU.mult)
                V.tensor_tensor(w(1), z[:, k, 1, :], z[:, k, 1, :], ALU.mult)
                done(V.scalar_tensor_tensor(out=z[:, k + 1, 1, :], in0=z[:, k, 0, :], scalar=2.0, in1=z[:, k, 1, :],
                                            op0=ALU.mult, op1=ALU.mult))
                done(V.tensor_tensor(z[:, k + 1, 0, :], w(0), w(1), ALU.subtract))
            base = steps[0]
            z_steps.append(base)
            per_chunk = 2 + 1 + 12
            with dve.Fori(0, CHUNKS // 2) as it:
                for n in range(2):
                    i0 = it * (2 * IC) + n * IC
                    at = lambda s, it=it, n=n: base + (it * 2 + n) * per_chunk + s
                    v, q, s = vb[n], qb[n], 3
                    c = cri[:].rearrange("p r (i c) -> p r i c", c=NCH)
                    dve.wait_ge(q_free[n], it + 1)
                    for r in range(2):
                        gg = ng[:, r, bass.ds(i0, IC)].unsqueeze(1).unsqueeze(3).to_broadcast([128, 2, IC, NCH])
                        last = V.tensor_tensor(tc[:, r], c[:, :, bass.ds(i0, IC), :], gg, ALU.mult)
                    last.then_inc(dve_step, 1)
                    dve.wait_ge(dve_step, at(1))
                    V.tensor_tensor(q[:, 0, :, 0:NCH], tc[:, 1, 1], tc[:, 0, 0], ALU.subtract)
                    V.tensor_tensor(q[:, 1, :, 0:NCH], tc[:, 0, 1], tc[:, 1, 0], ALU.add).then_inc(dve_step, 1)
                    dve.wait_ge(dve_step, at(2))
                    dve.wait_ge(v_free[n], it + 1)
                    V.memset(v[:, 0, :, 0:1], 1.0)
                    V.memset(v[:, 1, :, 0:1], 0.0).then_inc(dve_step, 1)
                    dve.wait_ge(dve_step, at(s))
                    for k in range(6):
                        m = 1 << k
                        old = v[:, :, :, 0:m]
                        for r in range(2):
                            zz = z[:, k, r, bass.ds(i0, IC)].unsqueeze(1).unsqueeze(3).to_broadcast([128, 2, IC, m])
                            last = V.tensor_tensor(tv[:, r, :, :, 0:m], old, zz, ALU.mult)
                        s += 1
                        last.then_inc(dve_step, 1)
                        dve.wait_ge(dve_step, at(s))
                        V.tensor_tensor(v[:, 0, :, m:2 * m], tv[:, 0, 0, :, 0:m], tv[:, 1, 1, :, 0:m], ALU.subtract)
                        s += 1
                        V.tensor_tensor(v[:, 1, :, m:2 * m], tv[:, 0, 1, :, 0:m], tv[:, 1, 0, :, 0:m],
                                        ALU.add).then_inc(dve_step, 1)
                        dve.wait_ge(dve_step, at(s))

        @block.gpsimd
        def _(pool):
            P = nc.gpsimd
            per_chunk, c_chunk = 1 + 2 * 3, 15
            pool.wait_ge(dve_step, z_steps[0])
            with pool.Fori(0, CHUNKS // 2) as it:
                for n in range(2):
                    i0 = it * (2 * IC) + n * IC
                    at = lambda s, it=it, n=n: (it * 2 + n) * per_chunk + s
                    q, s = qb[n], 0
                    pool.wait_ge(dve_step, it * (2 * c_chunk) + z_steps[0] + n * c_chunk + 2)
                    for k in range(3):
                        m = NCH << k
                        old = q[:, :, :, 0:m]
                        for r in range(2):
                            zz = z[:, 6 + k, r, bass.ds(i0, IC)].unsqueeze(1).unsqueeze(3).to_broadcast([128, 2, IC, m])
                            last = P.tensor_tensor(tq[:, r, :, :, 0:m], old, zz, ALU.mult)
                        s += 1
                        last.then_inc(pool_step, 1)
                        pool.wait_ge(pool_step, at(s))
                        P.tensor_tensor(q[:, 0, :, m:2 * m], tq[:, 0, 0, :, 0:m], tq[:, 1, 1, :, 0:m], ALU.add)
                        s += 1
                        P.tensor_tensor(q[:, 1, :, m:2 * m], tq[:, 0, 1, :, 0:m], tq[:, 1, 0, :, 0:m],
                                        ALU.subtract).then_inc(pool_step, 1)
                        pool.wait_ge(pool_step, at(s))
                    pool.sem_inc(pool_step, 1)

        @block.tensor
        def _(pe):
            base, v_chunk, q_chunk = z_steps[0], 15, 7
            for n in range(2):
                pe.sem_inc(v_free[n], 1)
                pe.sem_inc(q_free[n], 1)
            with pe.Fori(0, CHUNKS // 2) as it:
                for n in range(2):
                    pe.wait_ge(dve_step, it * (2 * v_chunk) + base + (n + 1) * v_chunk)
                    pe.wait_ge(pool_step, it * (2 * q_chunk) + (n + 1) * q_chunk)
                    pe.wait_ge(ps_free[n], it + 1)
                    pe.sem_inc(turn, 1)
                    for i in range(IC):
                        for p in range(2):
                            h = slice(64 * p, 64 * p + 64)
                            for r in range(2):
                                last = nc.tensor.matmul(ps[n][h, i, :], qb[n][h, r, i, :], vb[n][h, r, i, :],
                                                        start=(r == 0), stop=(r == 1))
                    last.then_inc(prod_ready, 1)
                    pe.wait_ge(prod_ready, it * 2 + n + 1)
                    pe.sem_inc(v_free[n], 1)
                    pe.sem_inc(q_free[n], 1)


def attention_inputs(nc, ctx, T, H):
    shapes = {
        "watt": [128, DM // 128, 6 * 128], "wo": [128, DM // 128, DM], "battn": [128, 6], "bo": [128, DM],
        "ident": [128, 128], "mask": [128, 128],
        "selh": [128, 4, 128],
        "selv": [128, 4, 128],
        "quad": [128, 4],
    }
    tiles = {n: ctx.enter_context(nc.sbuf_tensor("at_" + n, s, mybir.dt.float32)) for n, s in shapes.items()}
    loads = [(t[:], T[n].partition_broadcast(128) if n == "bo" else T[n]) for n, t in tiles.items()]
    return tuple(tiles.values()), loads + [(H[:, NT - 1, :], T["cls"].partition_broadcast(128))]


def attention_stage(nc, T, H, inputs):
    f32, bf16, fr = mybir.dt.float32, mybir.dt.bfloat16, mybir.dt.float32r
    ALU, ACT, AX = mybir.AluOpType, mybir.ActivationFunctionType, mybir.AxisListType
    KC = DM // 128
    NB = 4
    STEPS = 2 * NB
    ITERS = NCH // NB
    GROUPS = 4 * STEPS
    NK = 1 + 2 * 128
    CLS = 2 * NCH
    SCALE = float(HD) ** -0.5

    def tp_order():
        for n in range(STEPS):
            if n % 2 == 0:
                yield from (("x", n // 2, 0), ("x", n // 2, 1), ("v", n // 2, 0))
            for j in range(4):
                g = 4 * n + j - 1
                if g >= 0:
                    yield from (("p", g, kc) for kc in range(1 + (g // 4) % 2))
                if j == 1 and n > 0:
                    yield ("r", n - 1, 0)
        yield from (("p", GROUPS - 1, 0), ("p", GROUPS - 1, 1), ("r", STEPS - 1, 0))

    TP = {use: k for k, use in enumerate(tp_order())}
    TP_USES = len(TP) // 2
    assert len(TP) % 2 == 0

    def qk_order():
        for n in range(STEPS):
            if n % 2 == 0:
                yield from (("qkv", n // 2, m) for m in range(6))
            if n > 0:
                yield from (("rb", n - 1, 0), ("pr", n - 1, 0))
        yield from (("rb", STEPS - 1, 0), ("pr", STEPS - 1, 0))

    QK = {use: k for k, use in enumerate(qk_order())}
    QK_USES = len(QK)

    with ExitStack() as ctx:
        sb = lambda name, shape, dt=f32: ctx.enter_context(nc.sbuf_tensor("at_" + name, shape, dt))
        pb = lambda name, shape, dt=f32: ctx.enter_context(nc.psum_tensor("at_" + name, shape, dt))
        sem = lambda name: ctx.enter_context(nc.semaphore("at_" + name))
        watt, wo, bias, bo, ident, maskf, selh, selv, quad = inputs
        identb = sb("identb", [128, 128], bf16)
        maskb = sb("maskb", [128, 128], bf16)
        power = sb("power", [128, 1])
        st6 = sb("st6", [128, 2, 6])
        mv = sb("mv", [128, 2, 2])
        ve = sb("ve", [128, 2])
        rstd = sb("rstd", [128, 2])
        xn = sb("xn", [128, 2, DM])
        wh, wl = sb("wh", [128, KC, 6 * 128], fr), sb("wl", [128, KC, 6 * 128], fr)
        oh, ol = sb("oh", [128, KC, DM], fr), sb("ol", [128, KC, DM], fr)
        xh, xl = sb("xh", [128, KC, 256], fr), sb("xl", [128, KC, 256], fr)
        qh, ql = sb("qh", [128, 2, 4, 128], fr), sb("ql", [128, 2, 4, 128], fr)
        kh, kl = sb("kh", [128, 2, 4, NK + 1], fr), sb("kl", [128, 2, 4, NK + 1], fr)
        kp = sb("kp", [128, 2, NK + 1], fr)
        kz = sb("kz", [128, 2, 4, 1 + 128])
        ch, cl = sb("ch", [128, 512], fr), sb("cl", [128, 512], fr)
        xT = sb("xT", [128, KC, 128])
        qT = sb("qT", [128, 2, 4, 256])
        kT = sb("kT", [128, 2, NK + 1])
        vT = sb("vT", [128, 256])
        vtok = sb("vtok", [128, 2, 2, HD])
        v0 = sb("v0", [128, 128])
        nmax = sb("nmax", [128, 4])
        pg = sb("pg", [128, 2, 4, NK])
        pt = sb("pt", [128, 4, 3, 512])
        r2 = sb("r2", [128, 2, 128])
        rp = sb("rp", [128, 2, 128])
        rb = sb("rb", [128, 512])
        ctxT = sb("ctxT", [128, 512])
        S = [pb(f"S{m}", [128, 512]) for m in range(4)]
        tp = [pb(f"tp{k}", [128, 512]) for k in range(2)]
        qk = pb("qk", [128, 512])
        cx = pb("cx", [128, 512])
        banks = (qk, cx)
        dve_step, act_step, pool_step = sem("dve_step"), sem("act_step"), sem("pool_step")
        var_ready, rstd_ready = sem("var_ready"), sem("rstd_ready")
        xn_ready = sem("xn_ready")
        hb_ready = sem("hb_ready")
        tp_full = [sem(f"tp_full{k}") for k in range(2)]
        tp_free = [sem(f"tp_free{k}") for k in range(2)]
        qk_full, qk_free = sem("qk_full"), sem("qk_free")
        sc_full, max_done, exp_done = sem("sc_full"), sem("max_done"), sem("exp_done")
        pg_read, p0_done = sem("pg_read"), sem("p0_done")
        rec_ready = sem("rec_ready")
        pv_done, ctx_ready = sem("pv_done"), sem("ctx_ready")
        wh_ready, wl_ready, xh_ready = sem("wh_ready"), sem("wl_ready"), sem("xh_ready")
        high_ready, keys_ready, ch_ready, ctx_split = sem("high_ready"), sem("keys_ready"), sem("ch_ready"), sem("ctx_split")
        stats, aggr = sem("stats"), sem("aggr")
        load = [sem(f"load{k}") for k in range(4)]
        tile_ready = sem("tile_ready")
        cls_step = sem("cls_step")
        turn, dve_turn, pool_turn = sem("turn"), sem("dve_turn"), sem("pool_turn")

        def transposed(it, use):
            k = TP[use]
            return k % 2, it * TP_USES + k // 2 + 1

        with nc.Block() as block:

            @block.sync
            def _(sp):
                for t in range(2 * NCH):
                    c, p = t // 2, t % 2
                    src = T["hs"].rearrange("(p a c) i b -> p c i a b", p=2, c=NCH)[p, c]
                    dst = H[:, t, :].rearrange("i (a b) -> i a b", b=src.shape[2])
                    if t >= 4:
                        sp.wait_ge(load[t % 4], 16 * (t // 4))
                        sp.sem_inc(tile_ready, 1)
                    sp.dma_start(dst, src).then_inc(load[t % 4], 16)
                for n in range(4):
                    sp.wait_ge(load[n], 16 * NCH // 2)
                    sp.sem_inc(tile_ready, 1)

            @block.tensor
            def _(pe):
                pe.wait_ge(xn_ready, 1)
                for kc in range(KC):
                    last = nc.tensor.transpose(tp[0][:, kc * 128:(kc + 1) * 128], xn[:, 0, kc * 128:(kc + 1) * 128], ident[:])
                last.then_inc(cls_step, 1)
                pe.wait_ge(act_step, 1)
                for m in (4, 5):
                    for kc in range(KC):
                        last = nc.tensor.matmul(qk[:, (m - 4) * 128:(m - 3) * 128], watt[:, kc, m * 128:(m + 1) * 128],
                                                xT[:, kc, 0:128], start=(kc == 0), stop=(kc == KC - 1))
                last.then_inc(cls_step, 1)
                pe.wait_ge(act_step, 3)
                nc.tensor.transpose(tp[0][:, 0:128], v0[:], ident[:]).then_inc(cls_step, 1)
                for g in range(4):
                    last = nc.tensor.matmul(qk[:], v0[:], wo[:, g, :], start=(g == 0), stop=(g == 3))
                last.then_inc(cls_step, 1)
                pe.wait_ge(dve_step, 4)
                pe.wait_ge(wl_ready, 2)
                with pe.Fori(0, ITERS) as it:
                    def project_in(b):
                        for p in range(2):
                            bank, uses = transposed(it, ("x", b, p))
                            pe.wait_ge(xn_ready, it * (2 * NB) + 2 * b + p + 2)
                            pe.wait_ge(tp_free[bank], uses)
                            for kc in range(KC):
                                last = nc.tensor.transpose(tp[bank][:, kc * 128:(kc + 1) * 128],
                                                           xn[:, p, kc * 128:(kc + 1) * 128], ident[:])
                            last.then_inc(tp_full[bank], 1)
                        for p in range(2):
                            bank, uses = transposed(it, ("x", b, p))
                            pe.wait_ge(tp_free[bank], uses + 1)
                        pe.wait_ge(ctx_ready, it * STEPS + 2 * b + (1 if b == 0 else 0))
                        for m in range(6):
                            pe.wait_ge(qk_free, it * QK_USES + QK[("qkv", b, m)] + (1 if m == 0 else 0) + 1)
                            for kc in range(KC):
                                for w_, x_ in ((wh, xh), (wh, xl), (wl, xh)):
                                    last = nc.tensor.matmul(banks[m % 2][:, 0:256],
                                                            w_[:, kc, m * 128:(m + 1) * 128], x_[:, kc, :],
                                                            start=(kc == 0 and x_ is xh and w_ is wh),
                                                            stop=(kc == KC - 1 and w_ is wl))
                            last.then_inc(qk_full, 1)
                        bank, uses = transposed(it, ("v", b, 0))
                        pe.wait_ge(qk_free, it * QK_USES + QK[("qkv", b, 5)] + 3)
                        pe.wait_ge(tp_free[bank], uses)
                        for p in range(2):
                            last = nc.tensor.transpose(tp[bank][:, 128 * p:128 * p + 128],
                                                       vT[:, 128 * p:128 * p + 128], ident[:])
                        last.then_inc(tp_full[bank], 1)

                    def scores(n, j):
                        b, p, g = n // 2, n % 2, 4 * n + j
                        for m in range(4):
                            pe.wait_ge(exp_done, it * (4 * GROUPS) + 4 * g + m + 1)
                            if p == 1 and j == 0 and m == 0:
                                pe.wait_ge(keys_ready, it * (2 * NB) + 2 * b + 2)
                            pe.sem_inc(turn, 1)
                            keys = 129 if p == 0 else NK
                            if p == 0:
                                nc.tensor.matmul(S[m][:, 0:keys], qT[:, b % 2, m, 0:128], kz[:, b % 2, j, :],
                                                 start=True, stop=False, skip_group_check=True)
                            else:
                                for q_, k_ in ((qh, kh), (qh, kl), (ql, kh)):
                                    nc.tensor.matmul(S[m][:, 0:keys + 1], q_[:, b % 2, m, :], k_[:, b % 2, j, :],
                                                     start=(q_ is qh and k_ is kh), stop=False, skip_group_check=True)
                            nc.tensor.matmul(S[m][:, keys - 128:keys], identb[:], maskb[:], start=False, stop=True,
                                             skip_group_check=True).then_inc(sc_full, 1)

                    def transpose_probs(g):
                        n, j = divmod(g, 4)
                        pe.wait_ge(exp_done, it * (4 * GROUPS) + 4 * g + 8)
                        for kc in range(1 + n % 2):
                            bank, uses = transposed(it, ("p", g, kc))
                            pe.wait_ge(tp_free[bank], uses)
                            for m in range(4):
                                last = nc.tensor.transpose(tp[bank][:, m * 128:(m + 1) * 128],
                                                           pg[:, g % 2, m, 1 + 128 * kc:129 + 128 * kc], ident[:])
                            last.then_inc(tp_full[bank], 1)
                        pe.wait_ge(tp_full[bank], uses)
                        pe.sem_inc(pg_read, 1)

                    def context(n):
                        b, p = n // 2, n % 2
                        bank, uses = transposed(it, ("r", n, 0))
                        pe.wait_ge(rec_ready, it * STEPS + n + 1)
                        pe.wait_ge(p0_done, it * GROUPS + 4 * n + 6)
                        pe.wait_ge(tp_free[bank], uses)
                        pe.sem_inc(turn, 1)
                        nc.tensor.transpose(tp[bank][:, 0:128], r2[:, n % 2, :], ident[:]).then_inc(tp_full[bank], 1)
                        for k in range(2):
                            last = max(TP[("p", 4 * n + j, kc)] for j in range(4) for kc in range(1 + p)
                                       if TP[("p", 4 * n + j, kc)] % 2 == k)
                            pe.wait_ge(tp_free[k], it * TP_USES + last // 2 + 2)
                        pe.wait_ge(ctx_ready, it * STEPS + n + 1)
                        pe.sem_inc(turn, 1)
                        for kc in range(1 + p):
                            for j in range(4):
                                nc.tensor.matmul(cx[32 * j:32 * j + 32, :], vtok[:, b % 2, kc, :], pt[:, j, n % 2 + kc, :],
                                                 start=(kc == 0), stop=False, skip_group_check=True)
                        pe.wait_ge(tp_free[bank], uses + 1)
                        pe.wait_ge(qk_free, it * QK_USES + QK[("rb", n, 0)] + 2)
                        pe.sem_inc(turn, 1)
                        for m in range(4):
                            last = nc.tensor.matmul(cx[:, m * 128:(m + 1) * 128], selv[:, m, :], rp[:, n % 2, :],
                                                    start=False, stop=True, skip_group_check=True)
                        last.then_inc(pv_done, 1)
                        for m in range(4):
                            last = nc.tensor.matmul(qk[:, m * 128:(m + 1) * 128], selh[:, m, :], rp[:, n % 2, :],
                                                    start=(m == 0), stop=True, skip_group_check=True)
                        last.then_inc(qk_full, 1)

                    def project_out(n):
                        pe.wait_ge(ctx_split, it * STEPS + n + 2)
                        pe.wait_ge(qk_free, it * QK_USES + QK[("pr", n, 0)] + 2)
                        pe.sem_inc(turn, 1)
                        for m in range(4):
                            for c_, o_ in ((ch, oh), (ch, ol), (cl, oh)):
                                last = nc.tensor.matmul(qk[:], c_[:, m * 128:(m + 1) * 128], o_[:, m, :],
                                                        start=(m == 0 and c_ is ch and o_ is oh), stop=(m == 3 and c_ is cl))
                        last.then_inc(qk_full, 1)

                    for n in range(STEPS):
                        if n % 2 == 0:
                            project_in(n // 2)
                        for j in range(4):
                            scores(n, j)
                            if 4 * n + j > 0:
                                transpose_probs(4 * n + j - 1)
                            if j == 1 and n > 0:
                                context(n - 1)
                            if j == 3 and n > 0:
                                project_out(n - 1)
                    transpose_probs(GROUPS - 1)
                    context(STEPS - 1)
                    project_out(STEPS - 1)

            @block.scalar
            def _(act):
                A = nc.scalar
                A.copy(wh[:], watt[:]).then_inc(wh_ready, 1)
                A.copy(oh[:], wo[:]).then_inc(wh_ready, 1)
                act.wait_ge(cls_step, 1)
                A.copy(xT[:], tp[0][:].rearrange("p (k t) -> p k t", k=KC)).then_inc(act_step, 1)
                act.wait_ge(cls_step, 2)
                act.wait_ge(pool_step, 2)
                act.wait_ge(dve_step, 1)
                for b in range(2):
                    for j in range(4):
                        rows = slice(32 * j, 32 * j + 32)
                        A.activation(kz[rows, b, j, 0:1], qk[rows, 0:1], ACT.Identity, bias=bias[rows, 4:5])
                A.activation(kT[:, 0, 0:1], qk[:, 0:1], ACT.Identity, bias=bias[:, 4:5])
                A.activation(kT[:, 1, 0:1], qk[:, 0:1], ACT.Identity, bias=bias[:, 4:5]).then_inc(act_step, 1)
                A.activation(v0[:], qk[:, 128:256], ACT.Identity, bias=bias[:, 5:6]).then_inc(act_step, 1)
                act.wait_ge(dve_step, 4)
                act.sem_inc(tp_free[0], 1)
                act.sem_inc(exp_done, 4)
                with act.Fori(0, ITERS) as it:
                    def evacuate(use, dst, view):
                        bank, uses = transposed(it, use)
                        if bank == 0:
                            act.wait_ge(tp_full[0], uses)
                            A.copy(dst, view(tp[0])).then_inc(tp_free[0], 1)

                    def project_in(b):
                        for p in range(2):
                            bank, uses = transposed(it, ("x", b, p))
                            act.wait_ge(tp_full[bank], uses)
                            A.copy(xh[:, :, 128 * p:128 * p + 128],
                                   tp[bank][:].rearrange("p (k t) -> p k t", k=KC)).then_inc(xh_ready, 1)
                        for m in range(6):
                            act.wait_ge(qk_full, it * QK_USES + QK[("qkv", b, m)] + 1)
                            src = banks[m % 2][:, 0:256]
                            if m == 0:
                                act.wait_ge(pv_done, it * STEPS + 2 * b + 1)
                            if m == 4:
                                for j in range(4):
                                    rows = slice(32 * j, 32 * j + 32)
                                    A.activation(kz[rows, b % 2, j, 1:], banks[m % 2][rows, 0:128], ACT.Identity, bias=bias[rows, 4:5])
                            if m < 4:
                                A.activation(qT[:, b % 2, m, :], src, ACT.Identity, bias=bias[:, m:m + 1],
                                             scale=SCALE).then_inc(qk_free, 1)
                            else:
                                dst = kT[:, b % 2, 1:NK] if m == 4 else vT[:]
                                A.activation(dst, src, ACT.Identity, bias=bias[:, m:m + 1]).then_inc(qk_free, 1)
                        evacuate(("v", b, 0), vtok[:, b % 2], lambda t: t[:, 0:256].rearrange("p (k d) -> p k d", k=2)[:, :, 0:HD])

                    def probs(n, j):
                        g = 4 * n + j
                        act.wait_ge(pg_read, it * GROUPS + g + 1)
                        act.wait_ge(p0_done, it * GROUPS + g + 1)
                        for m in range(4):
                            keys = 129 if n % 2 == 0 else NK
                            act.wait_ge(max_done, it * (4 * GROUPS) + 4 * g + m + 1)
                            if m == 0 and j == 0:
                                act.wait_ge(pv_done, it * STEPS + n + 1)
                            A.activation(pg[:, g % 2, m, 0:keys], S[m][:, 0:keys], ACT.Exp, bias=nmax[:, m:m + 1],
                                         accum_out=r2[:, n % 2, 4 * j + m:4 * j + m + 1]).then_inc(exp_done, 1)

                    def take_probs(g):
                        n, j = divmod(g, 4)
                        for kc in range(1 + n % 2):
                            if j == 0 and kc == 0:
                                act.wait_ge(pv_done, it * STEPS + n + 1)
                            evacuate(("p", g, kc), pt[:, j, n % 2 + kc, :], lambda t: t[:])

                    def context(n):
                        evacuate(("r", n, 0), rp[:, n % 2, :], lambda t: t[:, 0:128])
                        act.wait_ge(qk_full, it * QK_USES + QK[("rb", n, 0)] + 1)
                        act.wait_ge(ctx_ready, it * STEPS + n + 1)
                        A.copy(rb[:], qk[:]).then_inc(qk_free, 1)

                    def split_context(n):
                        act.wait_ge(ctx_ready, it * STEPS + n + 2)
                        A.copy(ch[:], ctxT[:]).then_inc(ch_ready, 1)

                    for n in range(STEPS):
                        if n % 2 == 0:
                            project_in(n // 2)
                        for j in range(4):
                            probs(n, j)
                            if 4 * n + j > 0:
                                take_probs(4 * n + j - 1)
                            if j == 1 and n > 0:
                                context(n - 1)
                            if j == 2 and n > 0:
                                split_context(n - 1)
                    take_probs(GROUPS - 1)
                    context(STEPS - 1)
                    split_context(STEPS - 1)

            @block.vector
            def _(dve):
                V = nc.vector
                V.tensor_copy(identb[:], ident[:])
                V.tensor_copy(maskb[:], maskf[:])
                V.memset(r2[:], 0.0)
                V.memset(kT[:, :, NK:], 0.0)
                V.memset(kz[:], 0.0)
                V.memset(power[:], -0.5).then_inc(dve_step, 1)

                def moments(tiles, count):
                    for q, h in enumerate(tiles):
                        V.bn_stats(st6[:, q, :], h).then_inc(stats, 1)
                    dve.wait_ge(stats, count)
                    dve.sem_inc(dve_turn, 1)
                    for q in range(len(tiles)):
                        V.bn_aggr(mv[:, q, :], st6[:, q, :]).then_inc(aggr, 1)
                    dve.wait_ge(aggr, count)
                    dve.sem_inc(dve_turn, 1)
                    V.tensor_scalar(ve[:, 0:len(tiles)], mv[:, 0:len(tiles), 1], 1.0, EPS, ALU.mult, ALU.add).then_inc(var_ready, 1)

                def normalize(q, h):
                    V.tensor_scalar(xn[:, q, :], h, mv[:, q, 0:1], rstd[:, q:q + 1], ALU.subtract, ALU.mult).then_inc(xn_ready, 1)

                moments([H[:, CLS, :]], 1)
                dve.wait_ge(rstd_ready, 1)
                normalize(0, H[:, CLS, :])
                dve.wait_ge(wh_ready, 1)
                V.tensor_tensor(wl[:], watt[:], wh[:].bitcast(f32), ALU.subtract).then_inc(wl_ready, 1)
                dve.wait_ge(cls_step, 3)
                V.tensor_tensor(selv[32:48], selv[32:48], tp[0][32:48, 0:128].unsqueeze(1).to_broadcast([16, 4, 128]),
                                ALU.mult).then_inc(dve_step, 1)
                dve.wait_ge(cls_step, 4)
                V.tensor_tensor(H[:, CLS, :], H[:, CLS, :], bo[:], ALU.add).then_inc(dve_step, 1)
                dve.wait_ge(dve_step, 3)
                V.tensor_tensor(H[:, CLS, :], H[:, CLS, :], qk[:], ALU.add).then_inc(dve_step, 1)
                dve.sem_inc(tp_free[1], 1)
                dve.wait_ge(dve_step, 4)
                dve.sem_inc(qk_free, 2)
                dve.sem_inc(ctx_ready, 1)
                with dve.Fori(0, ITERS) as it:
                    def evacuate(use, dst, view):
                        bank, uses = transposed(it, use)
                        if bank == 1:
                            dve.wait_ge(tp_full[1], uses)
                            V.tensor_copy(dst, view(tp[1])).then_inc(tp_free[1], 1)

                    def tile(b, p):
                        return H[:, bass.ds(it * (2 * NB) + 2 * b + p, 1), :].rearrange("q o d -> q (o d)")

                    def batch_moments(b):
                        k = it * (2 * NB) + 2 * b
                        dve.wait_ge(tile_ready, k + 2)
                        dve.wait_ge(xn_ready, k + 1)
                        dve.sem_inc(dve_turn, 1)
                        moments([tile(b, 0), tile(b, 1)], k + 3)

                    def rows(b):
                        k = it * (2 * NB) + 2 * b
                        dve.wait_ge(rstd_ready, it * NB + b + 2)
                        for p in range(2):
                            if b == 0:
                                dve.wait_ge(cls_step, 1)
                            else:
                                bank, uses = transposed(it, ("x", b - 1, p))
                                dve.wait_ge(tp_full[bank], uses)
                            dve.sem_inc(dve_turn, 1)
                            normalize(p, tile(b, p))

                    def first_column(g):
                        n, j = divmod(g, 4)
                        if j == 0:
                            dve.wait_ge(pv_done, it * STEPS + n + 1)
                        dve.wait_ge(exp_done, it * (4 * GROUPS) + 4 * g + 8)
                        dve.sem_inc(dve_turn, 1)
                        V.tensor_copy(r2[:, n % 2, 32 + 4 * j:36 + 4 * j],
                                      pg[:, g % 2, :, 0:1].rearrange("q m o -> q (m o)")).then_inc(p0_done, 1)

                    def project_in(b):
                        for p in range(2):
                            bank, uses = transposed(it, ("x", b, p))
                            dve.wait_ge(xh_ready, it * (2 * NB) + 2 * b + p + 1)
                            part = xh[:, :, 128 * p:128 * p + 128]
                            V.tensor_tensor(xl[:, :, 128 * p:128 * p + 128],
                                            tp[bank][:].rearrange("p (k t) -> p k t", k=KC), part.bitcast(f32),
                                            ALU.subtract).then_inc(tp_free[bank], 1)
                        evacuate(("v", b, 0), vtok[:, b % 2], lambda t: t[:, 0:256].rearrange("p (k d) -> p k d", k=2)[:, :, 0:HD])

                    def maxima(n, j):
                        g = 4 * n + j
                        for m in range(4):
                            keys = 129 if n % 2 == 0 else NK
                            dve.wait_ge(sc_full, it * (4 * GROUPS) + 4 * g + m + 1)
                            dve.wait_ge(exp_done, it * (4 * GROUPS) + 4 * g + m + 1)
                            V.tensor_reduce(out=nmax[:, m:m + 1], in_=S[m][:, 0:keys], axis=AX.X, op=ALU.max,
                                            negate=True).then_inc(max_done, 1)

                    def take_probs(g):
                        n, j = divmod(g, 4)
                        for kc in range(1 + n % 2):
                            if j == 0:
                                dve.wait_ge(pv_done, it * STEPS + n + 1)
                            evacuate(("p", g, kc), pt[:, j, n % 2 + kc, :], lambda t: t[:])

                    def reciprocals(n):
                        dve.wait_ge(exp_done, it * (4 * GROUPS) + 16 * n + 16 + 4)
                        V.reciprocal(r2[:, n % 2, 0:16], r2[:, n % 2, 0:16]).then_inc(rec_ready, 1)

                    def context(n):
                        evacuate(("r", n, 0), rp[:, n % 2, :], lambda t: t[:, 0:128])
                        dve.wait_ge(qk_free, it * QK_USES + QK[("rb", n, 0)] + 3)
                        dve.wait_ge(pv_done, it * STEPS + n + 3)
                        V.tensor_tensor(ctxT[:], cx[:], rb[:], ALU.mult).then_inc(ctx_ready, 1)

                    def split_context(n):
                        dve.wait_ge(ch_ready, it * STEPS + n + 1)
                        dve.sem_inc(dve_turn, 1)
                        V.tensor_tensor(cl[:], ctxT[:], ch[:].bitcast(f32), ALU.subtract).then_inc(ctx_split, 1)

                    def project_out(n):
                        k = it * STEPS + n
                        dve.wait_ge(qk_full, it * QK_USES + QK[("pr", n, 0)] + 1)
                        dve.wait_ge(hb_ready, k + 1)
                        h = H[:, bass.ds(k, 1), :].rearrange("q o d -> q (o d)")
                        V.tensor_tensor(h, h, qk[:], ALU.add).then_inc(qk_free, 1)

                    batch_moments(0)
                    rows(0)
                    for n in range(STEPS):
                        if n % 2 == 0:
                            project_in(n // 2)
                        for j in range(4):
                            maxima(n, j)
                            if j == 3 and n % 2 == 0 and n // 2 + 1 < NB:
                                batch_moments(n // 2 + 1)
                            if 4 * n + j > 0:
                                first_column(4 * n + j - 1)
                                take_probs(4 * n + j - 1)
                            if j == 0 and n > 0:
                                reciprocals(n - 1)
                            if j == 1 and n > 0:
                                context(n - 1)
                            if j == 2 and n > 0:
                                split_context(n - 1)
                            if j == 1 and n % 2 == 1 and n // 2 + 1 < NB:
                                rows(n // 2 + 1)
                            if j == 3 and n > 0:
                                project_out(n - 1)
                    first_column(GROUPS - 1)
                    take_probs(GROUPS - 1)
                    reciprocals(STEPS - 1)
                    context(STEPS - 1)
                    split_context(STEPS - 1)
                    project_out(STEPS - 1)

            @block.gpsimd
            def _(pool):
                P = nc.gpsimd
                def inverse_root(tiles, count):
                    pool.wait_ge(var_ready, count)
                    P.tensor_tensor(rstd[:, 0:tiles], ve[:, 0:tiles], power[:].to_broadcast([128, tiles]),
                                    ALU.pow).then_inc(rstd_ready, 1)

                P.tensor_scalar(bias[:, 0:4], bias[:, 0:4], SCALE, None, ALU.mult).then_inc(pool_step, 2)
                pool.wait_ge(dve_step, 1)
                inverse_root(1, 1)
                pool.wait_ge(wh_ready, 2)
                P.tensor_tensor(ol[:], wo[:], oh[:].bitcast(f32), ALU.subtract).then_inc(wl_ready, 1)
                pool.sem_inc(ctx_split, 1)
                pool.sem_inc(pg_read, 2)
                pool.sem_inc(p0_done, 2)
                pool.sem_inc(pv_done, 2)
                with pool.Fori(0, ITERS) as it:
                    def rows(b):
                        for p in range(2):
                            k = it * (2 * NB) + 2 * b + p
                            pool.wait_ge(xn_ready, k + 2)
                            pool.sem_inc(pool_turn, 1)
                            h = H[:, bass.ds(k, 1), :].rearrange("q o d -> q (o d)")
                            P.tensor_tensor(h, h, bo[:], ALU.add).then_inc(hb_ready, 1)

                    def split_keys(b):
                        pool.wait_ge(qk_free, it * QK_USES + QK[("qkv", b, 5)] + 3)
                        pool.sem_inc(pool_turn, 1)
                        P.tensor_copy(qh[:, b % 2], qT[:, b % 2, :, 128:256]).then_inc(high_ready, 1)
                        P.tensor_copy(kp[:, 0], kT[:, b % 2]).then_inc(high_ready, 1)
                        pool.wait_ge(high_ready, it * (3 * NB) + 3 * b + 2)
                        pool.sem_inc(pool_turn, 1)
                        P.tensor_tensor(ql[:, b % 2], qT[:, b % 2, :, 128:256], qh[:, b % 2].bitcast(f32), ALU.subtract)
                        P.tensor_tensor(kp[:, 1], kT[:, b % 2], kp[:, 0].bitcast(f32), ALU.subtract).then_inc(high_ready, 1)
                        pool.wait_ge(high_ready, it * (3 * NB) + 3 * b + 3)
                        pool.sem_inc(pool_turn, 1)
                        for part, k_ in enumerate((kh, kl)):
                            P.tensor_tensor(k_[:, b % 2], kp[:, part].bitcast(f32).unsqueeze(1).to_broadcast([128, 4, NK + 1]),
                                            quad[:].unsqueeze(2).to_broadcast([128, 4, NK + 1]), ALU.mult).then_inc(keys_ready, 1)
                        pool.wait_ge(keys_ready, it * (2 * NB) + 2 * b + 2)

                    for b in range(NB):
                        inverse_root(2, it * NB + b + 2)
                        rows(b)
                        split_keys(b)


def route_stage(nc, T, H, slot_info, slot_rows):
    f32, bf16, i32, u32 = mybir.dt.float32, mybir.dt.bfloat16, mybir.dt.int32, mybir.dt.uint32
    ALU, ACT, AX = mybir.AluOpType, mybir.ActivationFunctionType, mybir.AxisListType
    KC = DM // 128
    FC = FF // 128
    CLS = NT - 1
    GROUPS = [list(range(t, min(t + 4, NT))) for t in range(0, NT, 4)]
    STATS = [range(t, min(t + 6, NT)) for t in range(0, NT, 6)]
    SB = 6
    TERMS = 8
    NE = NEXP

    with ExitStack() as ctx:
        sb = lambda name, shape, dt=f32: ctx.enter_context(nc.sbuf_tensor("rt_" + name, shape, dt))
        sem = lambda name: ctx.enter_context(nc.semaphore("rt_" + name))
        ident = sb("ident", [128, 128])
        upf = sb("upf", [128, 128])
        upper = sb("upper", [128, 128], bf16)
        onesb = sb("onesb", [128, 128], bf16)
        iota = sb("iota", [128, 128])
        rowid = sb("rowid", [128, 1])
        isrow = sb("isrow", [128, 1])
        rw = sb("rw", [128, KC, NE])
        eb = sb("eb", [128, NE])
        sgu = sb("sgu", [128, KC, 2 * FF])
        sdn = sb("sdn", [128, FC, DM])
        mhalf = sb("mhalf", [128, 1])
        zero = sb("zero", [128, DM + NE])
        st6 = sb("st6", [128, NT, 6])
        mv = sb("mv", [128, NT, 2])
        ve = sb("ve", [128, NT])
        rstd = sb("rstd", [128, NT])
        spare = sb("spare", [128, 1])
        xa = sb("xa", [128, NT, DM + NE])
        xT = sb("xT", [128, KC, NT * 128])
        lT = sb("lT", [NE, 512])
        L = sb("L", [128, NT, NE])
        w = [sb(f"w{k}", [128, NT, NE]) for k in range(4)]
        score = sb("score", [128, NT, NE])
        top = sb("top", [128, NT, 8])
        topi = sb("topi", [128, NT, 8], u32)
        topf = sb("topf", [128, NT, 8])
        pick = sb("pick", [128, NT, 4, NE], bf16)
        mask = sb("mask", [128, NT, NE], bf16)
        tsum = sb("tsum", [128, NT, 1])
        cnt = sb("cnt", [128, 6, NE])
        cnti = sb("cnti", [128, NE], i32)
        pos = sb("pos", [128, NT, 4])
        posi = sb("posi", [128, 3, NT * 4], i32)
        posf = sb("posf", [128, 2, NT, 4])
        rowsel = sb("rowsel", [128, SB, 4, 128], bf16)
        slotsel = sb("slotsel", [128, SB, 4, 2, NS], bf16)
        eqs = sb("eqs", [128, 4, NS])
        info = sb("info", [128, 3, NE])
        infoc = sb("infoc", [128, 2])
        infor = sb("infor", [1, 5, 128])
        infoi = sb("infoi", [1, 128], i32)
        tabf = sb("tabf", [128, 3, NS])
        sil = sb("sil", [128, FC, 512])
        gc = sb("gc", [128, FC, 512])
        uc = sb("uc", [128, FC, 512])
        actT = [sb(f"actT{n}", [128, FC, 512]) for n in range(2)]
        bank = [ctx.enter_context(nc.psum_tensor(f"rt_p{k}", [128, 512], f32)) for k in range(8)]
        tx, lg, lt = bank[0:2], bank[2], bank[3]
        gu = bank[0:4]
        rank = bank[6:8]
        yb = bank[4:6]
        tab, rowp = bank[6], bank[7]

        in_ready, w_ready, zero_done, x2_done, acc_done = (sem(n) for n in ("in_ready", "w_ready", "zero_done", "x2_done", "acc_done"))
        dve_step = sem("dve_step")
        var_ready, rstd_ready, xn_ready = sem("var_ready"), sem("rstd_ready"), sem("xn_ready")
        tx_full, tx_taken = sem("tx_full"), sem("tx_taken")
        lg_full, lg_taken, lt_full, lt_taken = sem("lg_full"), sem("lg_taken"), sem("lt_full"), sem("lt_taken")
        sp_ready, root_ready = sem("sp_ready"), sem("root_ready")
        probs_ready, mask_ready, rank_full = sem("probs_ready"), sem("mask_ready"), sem("rank_full")
        pos_ready, rowsel_ready, slotsel_ready, table_used = sem("pos_ready"), sem("rowsel_ready"), sem("slotsel_ready"), sem("table_used")
        gu_full, gu_taken, gate_ready, silu_ready, act_ready = (sem(n) for n in ("gu_full", "gu_taken", "gate_ready", "silu_ready", "act_ready"))
        y_full, y_taken, down_done = sem("y_full"), sem("y_taken"), sem("down_done")
        info_ready, row_full, rank_read = sem("info_ready"), sem("row_full"), sem("rank_read")

        with nc.Block() as block:

            @block.sync
            def _(sp):
                for dst, name in ((ident[:], "ident"), (upf[:], "upper"), (iota[:], "iota"), (rowid[:], "rowid"), (isrow[:], "isrow")):
                    sp.dma_start(dst, T[name]).then_inc(in_ready, 16)
                sp.dma_start(rw[:], T["router"]).then_inc(in_ready, 16)
                sp.dma_start(eb[:], T["ebias"].partition_broadcast(128)).then_inc(in_ready, 16)
                sp.dma_start(sgu[:], T["sgu"]).then_inc(w_ready, 16)
                sp.dma_start(sdn[:], T["sdn"]).then_inc(w_ready, 16)
                sp.wait_ge(dve_step, 1)
                sp.dma_start(T["x2"][TOKENS:TOKENS + 128, :], zero[:]).then_inc(zero_done, 16)
                sp.dma_start(T["acc"][TOKENS:TOKENS + 128, :], zero[:, 0:DM]).then_inc(zero_done, 16)
                sp.wait_ge(probs_ready, 1)
                for t in range(NT):
                    n = 128 if t < CLS else TOKENS - 128 * CLS
                    sp.dma_start(T["x2"][128 * t:128 * t + n, :], xa[0:n, t, :]).then_inc(x2_done, 16)
                for t in range(NT):
                    n = 128 if t < CLS else TOKENS - 128 * CLS
                    sp.wait_ge(y_taken, t + 1)
                    sp.dma_start(T["acc"][128 * t:128 * t + n, :], H[0:n, t, :]).then_inc(acc_done, 16)
                sp.wait_ge(zero_done, 32)
                sp.wait_ge(x2_done, 16 * NT)
                sp.wait_ge(acc_done, 16 * NT)

            @block.tensor
            def _(pe):
                M = nc.tensor.matmul
                pe.wait_ge(in_ready, 7 * 16)
                def transpose_rows(q):
                    for t in GROUPS[q]:
                        pe.wait_ge(xn_ready, t + 1)
                        if t >= 2:
                            pe.wait_ge(tx_taken, t - 1)
                        for kc in range(KC):
                            last = nc.tensor.transpose(tx[t % 2][:, 128 * kc:128 * kc + 128],
                                                       xa[:, t, 128 * kc:128 * kc + 128], ident[:])
                        last.then_inc(tx_full, 1)

                def logits(q):
                    tiles = GROUPS[q]
                    n = 128 * len(tiles)
                    pe.wait_ge(tx_taken, tiles[-1] + 1)
                    if q:
                        pe.wait_ge(lg_taken, q)
                    for kc in range(KC):
                        last = M(lg[0:NE, 0:n], rw[:, kc, :], xT[:, kc, 128 * tiles[0]:128 * tiles[0] + n],
                                 start=(kc == 0), stop=(kc == KC - 1))
                    last.then_inc(lg_full, 1)

                def transpose_logits(q):
                    pe.wait_ge(lg_taken, q + 1)
                    if q:
                        pe.wait_ge(lt_taken, q)
                    for k in range(len(GROUPS[q])):
                        last = nc.tensor.transpose(lt[:, NE * k:NE * k + NE], lT[:, 128 * k:128 * k + 128], ident[0:NE, 0:NE])
                    last.then_inc(lt_full, 1)

                for q in range(len(GROUPS) + 2):
                    if q < len(GROUPS):
                        transpose_rows(q)
                    if q >= 2:
                        transpose_logits(q - 2)
                    if 1 <= q <= len(GROUPS):
                        logits(q - 1)
                pe.wait_ge(lt_taken, len(GROUPS))
                pe.wait_ge(w_ready, 32)

                def gate_up(q):
                    tiles = GROUPS[q]
                    n = 128 * len(tiles)
                    if q:
                        pe.wait_ge(gu_taken, q)
                    for m in range(2 * FC):
                        for kc in range(KC):
                            last = M(gu[m][:, 0:n], sgu[:, kc, 128 * m:128 * m + 128],
                                     xT[:, kc, 128 * tiles[0]:128 * tiles[0] + n], start=(kc == 0), stop=(kc == KC - 1))
                    last.then_inc(gu_full, 1)

                def down(q):
                    pe.wait_ge(act_ready, q + 1)
                    for k, t in enumerate(GROUPS[q]):
                        if t >= 2:
                            pe.wait_ge(y_taken, t - 1)
                        for c in range(FC):
                            last = M(yb[t % 2][:], actT[q % 2][:, c, 128 * k:128 * k + 128], sdn[:, c, :],
                                     start=(c == 0), stop=(c == FC - 1))
                        last.then_inc(y_full, 1)
                    pe.wait_ge(y_full, GROUPS[q][-1] + 1)
                    pe.sem_inc(down_done, 1)

                def table(tiles):
                    for t in tiles:
                        pe.wait_ge(rowsel_ready, t + 1)
                        pe.wait_ge(slotsel_ready, t + 1)
                        for k in range(4):
                            last = M(tab[:, 0:2 * NS], rowsel[:, t % SB, k, :], slotsel[:, t % SB, k].rearrange("p a s -> p (a s)"),
                                     start=(t == 0 and k == 0), stop=(t == NT - 1 and k == 3))
                        last.then_inc(table_used, 1)

                gate_up(0)
                gate_up(1)
                down(0)
                gate_up(2)
                pe.wait_ge(mask_ready, 1)
                flat = mask[:].rearrange("p t e -> p (t e)")
                M(rank[0][:], upper[:], flat[:, 0:512], start=True, stop=False, skip_group_check=True)
                for d in range(1, NT - 1):
                    M(rank[0][:, NE * d:512], onesb[:], flat[:, 0:512 - NE * d], start=False, stop=(d == NT - 2),
                      skip_group_check=True)
                M(rank[1][:, 0:NE], upper[:], mask[:, NT - 1, :], start=True, stop=False, skip_group_check=True)
                for t in range(NT - 1):
                    M(rank[1][:, 0:NE], onesb[:], mask[:, t, :], start=False, stop=(t == NT - 2), skip_group_check=True)
                for t in range(NT):
                    last = M(rank[1][:, NE:2 * NE], onesb[:], mask[:, t, :], start=False, stop=(t == NT - 1),
                             skip_group_check=True)
                last.then_inc(rank_full, 1)
                down(1)
                gate_up(3)
                down(2)
                pe.wait_ge(rank_read, 1)
                table(range(0, SB))
                gate_up(4)
                down(3)
                table(range(SB, 2 * SB))
                down(4)
                table(range(2 * SB, NT))
                pe.wait_ge(info_ready, 1)
                for k in range(2):
                    last = M(rowp[0:1, 128 * k:128 * k + 128], infoc[:, k:k + 1], ident[:], start=(k == 0), stop=True,
                             skip_group_check=True)
                last.then_inc(row_full, 1)

            @block.scalar
            def _(act):
                A = nc.scalar
                for q in range(len(GROUPS) + 2):
                    if q < len(GROUPS):
                        for t in GROUPS[q]:
                            act.wait_ge(tx_full, t + 1)
                            A.copy(xT[:, :, 128 * t:128 * t + 128],
                                   tx[t % 2][:].rearrange("p (k t) -> p k t", k=KC)).then_inc(tx_taken, 1)
                    if q >= 2:
                        tiles = GROUPS[q - 2]
                        act.wait_ge(lt_full, q - 1)
                        A.copy(L[:, tiles[0]:tiles[-1] + 1, :].rearrange("p t e -> p (t e)"),
                               lt[:, 0:NE * len(tiles)]).then_inc(lt_taken, 1)
                    if 1 <= q <= len(GROUPS):
                        n = 128 * len(GROUPS[q - 1])
                        act.wait_ge(lg_full, q)
                        A.copy(lT[:, 0:n], lg[0:NE, 0:n]).then_inc(lg_taken, 1)
                for q, tiles in enumerate(GROUPS):
                    n = 128 * len(tiles)
                    act.wait_ge(gate_ready, q + 1)
                    A.activation(sil[:, :, 0:n], gc[:, :, 0:n], ACT.Silu).then_inc(silu_ready, 1)
                    if q == 0:
                        act.wait_ge(sp_ready, 1)
                        A.activation(score[:].rearrange("p t e -> p (t e)"), w[2][:].rearrange("p t e -> p (t e)"),
                                     ACT.Sqrt).then_inc(root_ready, 1)

            @block.vector
            def _(dve):
                V = nc.vector
                steps = [0]

                def done(ins):
                    steps[0] += 1
                    ins.then_inc(dve_step, 1)
                    dve.wait_ge(dve_step, steps[0])

                def flat(t):
                    return t[:].rearrange("p t e -> p (t e)")

                V.memset(slot_info[:], 0)
                done(V.memset(zero[:], 0.0))
                V.memset(mhalf[:], -0.5)
                done(V.memset(onesb[:], 1.0))
                def moments(part):
                    for t in part:
                        V.bn_stats(st6[:, t, :], H[:, t, :]).then_inc(dve_step, 1)
                    steps[0] += len(part)
                    dve.wait_ge(dve_step, steps[0])
                    for t in part:
                        V.bn_aggr(mv[:, t, :], st6[:, t, :]).then_inc(dve_step, 1)
                    steps[0] += len(part)
                    dve.wait_ge(dve_step, steps[0])
                    V.tensor_scalar(ve[:, part[0]:part[-1] + 1], mv[:, part[0]:part[-1] + 1, 1], 1.0, EPS,
                                    ALU.mult, ALU.add).then_inc(var_ready, 1)

                def normalize(k):
                    dve.wait_ge(rstd_ready, k + 1)
                    for t in STATS[k]:
                        V.tensor_scalar(xa[:, t, 0:DM], H[:, t, :], mv[:, t, 0:1], rstd[:, t:t + 1],
                                        ALU.subtract, ALU.mult).then_inc(xn_ready, 1)

                for k in range(len(STATS) + 1):
                    if k < len(STATS):
                        moments(STATS[k])
                    if k >= 1:
                        normalize(k - 1)
                dve.wait_ge(in_ready, 7 * 16)
                V.tensor_copy(upper[:], upf[:])

                def clipped(q):
                    n = 128 * len(GROUPS[q])
                    dve.wait_ge(gu_full, q + 1)
                    if q:
                        dve.wait_ge(silu_ready, q)
                    for c in range(FC):
                        last = V.tensor_scalar(gc[:, c, 0:n], gu[c][:, 0:n], -ALPHA, ALPHA, ALU.max, ALU.min)
                    last.then_inc(gate_ready, 1)
                    for c in range(FC):
                        last = V.tensor_scalar(uc[:, c, 0:n], gu[FC + c][:, 0:n], -ALPHA, ALPHA, ALU.max, ALU.min)
                    last.then_inc(gu_taken, 1)
                    dve.wait_ge(gu_taken, q + 1)
                    dve.wait_ge(silu_ready, q + 1)
                    if q >= 2:
                        dve.wait_ge(down_done, q - 1)
                    V.tensor_tensor(actT[q % 2][:, :, 0:n], sil[:, :, 0:n], uc[:, :, 0:n], ALU.mult).then_inc(act_ready, 1)

                def add_shared(q, half):
                    for t in GROUPS[q][2 * half:2 * half + 2]:
                        dve.wait_ge(y_full, t + 1)
                        V.tensor_tensor(H[:, t, :], H[:, t, :], yb[t % 2][:], ALU.add).then_inc(y_taken, 1)

                def select_slots(tiles):
                    for t in tiles:
                        if t >= SB:
                            dve.wait_ge(table_used, t - SB + 1)
                        done(V.tensor_tensor(eqs[:], iota[:, 0:NS].unsqueeze(1).to_broadcast([128, 4, NS]),
                                             posf[:, 0, t, :].unsqueeze(2).to_broadcast([128, 4, NS]), ALU.is_equal))
                        done(V.tensor_scalar(slotsel[:, t % SB, :, 0, :], eqs[:], rowid[:], None, ALU.mult))
                        V.tensor_scalar(slotsel[:, t % SB, :, 1, :], eqs[:], float(t + 1), None, ALU.mult).then_inc(slotsel_ready, 1)
                        dve.wait_ge(slotsel_ready, t + 1)

                dve.wait_ge(lt_taken, len(GROUPS))
                e, s, s2, p = (flat(x) for x in w)
                scale = flat(w[2]).bitcast(i32)
                done(V.scalar_tensor_tensor(out=e, in0=flat(L), scalar=-1.0, in1=flat(L), op0=ALU.mult, op1=ALU.min))
                exponential(V, done, e, e, s, p, scale)
                done(V.tensor_scalar(s, e, 2.0, None, ALU.add))
                done(V.reciprocal(s2, s))
                done(V.tensor_tensor(s, e, s2, ALU.mult))
                done(V.tensor_tensor(s2, s, s, ALU.mult))
                clipped(0)
                done(V.tensor_scalar(p, s2, 1.0 / (2 * TERMS + 1), None, ALU.mult))
                for k in range(TERMS - 1, 0, -1):
                    done(V.scalar_tensor_tensor(out=p, in0=p, scalar=1.0 / (2 * k + 1), in1=s2, op0=ALU.add, op1=ALU.mult))
                done(V.scalar_tensor_tensor(out=p, in0=p, scalar=1.0, in1=s, op0=ALU.add, op1=ALU.mult))
                done(V.tensor_scalar(s, flat(L), 0.0, None, ALU.max))
                V.scalar_tensor_tensor(out=s2, in0=p, scalar=2.0, in1=s, op0=ALU.mult, op1=ALU.add).then_inc(sp_ready, 1)
                dve.wait_ge(root_ready, 1)
                done(V.tensor_scalar(s, flat(score), 1e-19, None, ALU.max))
                done(V.reciprocal(p, s))
                done(V.tensor_tensor(p, s2, p, ALU.mult))
                done(V.tensor_tensor(p, p, flat(score), ALU.add))
                done(V.tensor_scalar(flat(score), p, 0.5, None, ALU.mult))
                done(V.tensor_tensor(w[0][:], score[:], eb[:].unsqueeze(1).to_broadcast([128, NT, NE]), ALU.add))
                clipped(1)
                add_shared(0, 0)
                for t in range(NT):
                    V.max(top[:, t, :], w[0][:, t, :]).then_inc(dve_step, 1)
                steps[0] += NT
                dve.wait_ge(dve_step, steps[0])
                for t in range(NT):
                    V.max_index(topi[:, t, :], top[:, t, :], w[0][:, t, :]).then_inc(dve_step, 1)
                steps[0] += NT
                dve.wait_ge(dve_step, steps[0])
                done(V.tensor_copy(topf[:], topi[:]))
                for k in range(4):
                    V.tensor_tensor(pick[:, :, k, :], iota[:, 0:NE].unsqueeze(1).to_broadcast([128, NT, NE]),
                                    topf[:, :, k:k + 1].to_broadcast([128, NT, NE]), ALU.is_equal).then_inc(dve_step, 1)
                steps[0] += 4
                dve.wait_ge(dve_step, steps[0])
                add_shared(0, 1)
                cls_pick = pick[:, CLS].rearrange("p k e -> p (k e)")
                done(V.tensor_scalar(cls_pick, cls_pick, isrow[:], None, ALU.mult))
                V.tensor_tensor(w[1][:], pick[:, :, 0, :], pick[:, :, 1, :], ALU.add)
                done(V.tensor_tensor(w[2][:], pick[:, :, 2, :], pick[:, :, 3, :], ALU.add))
                done(V.tensor_tensor(w[3][:], w[1][:], w[2][:], ALU.add))
                V.tensor_copy(mask[:], w[3][:]).then_inc(mask_ready, 1)
                done(V.tensor_tensor(w[1][:], w[3][:], score[:], ALU.mult))
                done(V.tensor_reduce(out=tsum[:].rearrange("p t o -> p (t o)"), in_=w[1][:], axis=AX.X, op=ALU.add))
                done(V.tensor_scalar(tsum[:], tsum[:], 1e-20, None, ALU.add))
                done(V.reciprocal(tsum[:], tsum[:]))
                V.tensor_tensor(xa[:, :, DM:], w[1][:], tsum[:].to_broadcast([128, NT, NE]), ALU.mult).then_inc(probs_ready, 1)

                clipped(2)
                dve.wait_ge(rank_full, 1)
                n_, tiles_, end_, tmp_ = cnt[:, 0, :], cnt[:, 1, :], cnt[:, 2, :], cnt[:, 3, :]
                done(V.tensor_copy(n_, rank[1][:, NE:2 * NE]))
                done(V.tensor_scalar(cnti[:], n_, 127.0, None, ALU.add))
                done(V.tensor_scalar(cnti[:], cnti[:], 7, None, ALU.logical_shift_right))
                done(V.tensor_copy(tiles_, cnti[:]))
                src, dst = tiles_, end_
                for k in range(5):
                    d = 1 << k
                    V.tensor_copy(dst[:, 0:d], src[:, 0:d])
                    done(V.tensor_tensor(dst[:, d:], src[:, d:], src[:, :NE - d], ALU.add))
                    src, dst = dst, (tmp_ if dst is end_ else end_)
                end_ = src
                done(V.tensor_tensor(cnt[:, 4, :], end_, tiles_, ALU.subtract))
                done(V.tensor_scalar(cnt[:, 4, :], cnt[:, 4, :], 128.0, None, ALU.mult))
                V.tensor_tensor(w[0][:, 0:NT - 1, :], rank[0][:].rearrange("p (t e) -> p t e", e=NE),
                                cnt[:, 4, :].unsqueeze(1).to_broadcast([128, NT - 1, NE]), ALU.add)
                V.tensor_tensor(w[0][:, NT - 1, :], rank[1][:, 0:NE], cnt[:, 4, :], ALU.add).then_inc(rank_read, 1)
                dve.wait_ge(rank_read, 1)
                add_shared(1, 0)
                for k in range(4):
                    done(V.tensor_tensor(w[1][:], w[0][:], pick[:, :, k, :], ALU.mult))
                    done(V.tensor_reduce(out=pos[:, :, k:k + 1].rearrange("p t o -> p (t o)"), in_=w[1][:], axis=AX.X, op=ALU.add))
                add_shared(1, 1)
                pi = lambda k: posi[:, k, :]
                done(V.tensor_copy(pi(0), pos[:].rearrange("p t k -> p (t k)")))
                V.tensor_scalar(pi(1), pi(0), 7, None, ALU.logical_shift_right)
                done(V.tensor_scalar(pi(2), pi(0), 127, None, ALU.bitwise_and))
                V.tensor_copy(posf[:, 0].rearrange("p t k -> p (t k)"), pi(1))
                done(V.tensor_copy(posf[:, 1].rearrange("p t k -> p (t k)"), pi(2)))
                V.tensor_scalar(posf[:, 0, CLS, :], posf[:, 0, CLS, :], 1.0, isrow[:], ALU.add, ALU.mult).then_inc(dve_step, 1)
                steps[0] += 1
                dve.wait_ge(dve_step, steps[0])
                V.tensor_scalar(posf[:, 0, CLS, :], posf[:, 0, CLS, :], -1.0, None, ALU.add).then_inc(pos_ready, 1)
                dve.wait_ge(pos_ready, 1)
                V.tensor_scalar(info[:, 0, :], end_, rowid[:], None, ALU.is_le)
                done(V.tensor_scalar(info[:, 1, :], tiles_, 0.0, None, ALU.is_gt))
                done(V.tensor_tensor(info[:, 2, :], info[:, 0, :], info[:, 1, :], ALU.mult))
                V.tensor_reduce(out=infoc[:, 0:1], in_=info[:, 0, :], axis=AX.X, op=ALU.add)
                V.tensor_reduce(out=infoc[:, 1:2], in_=info[:, 2, :], axis=AX.X, op=ALU.add).then_inc(info_ready, 1)
                clipped(3)
                add_shared(2, 0)
                select_slots(range(0, SB))
                add_shared(2, 1)
                clipped(4)
                add_shared(3, 0)
                select_slots(range(SB, 2 * SB))
                add_shared(3, 1)
                select_slots(range(2 * SB, 2 * SB + 3))
                add_shared(4, 0)
                select_slots(range(2 * SB + 3, NT))
                dve.wait_ge(table_used, NT)
                V.tensor_scalar(tabf[:, 0, :], tab[:, NS:2 * NS], 0.0, None, ALU.is_equal)
                done(V.tensor_scalar(tabf[:, 1, :], tab[:, NS:2 * NS], 128.0, -128.0, ALU.mult, ALU.add))
                done(V.tensor_tensor(tabf[:, 1, :], tabf[:, 1, :], tab[:, 0:NS], ALU.add))
                V.tensor_scalar(spare[:], rowid[:], float(TOKENS + 128), None, ALU.add).then_inc(dve_step, 1)
                steps[0] += 1
                dve.wait_ge(dve_step, steps[0])
                done(V.scalar_tensor_tensor(out=tabf[:, 2, :], in0=tabf[:, 0, :], scalar=spare[:], in1=tabf[:, 1, :],
                                            op0=ALU.mult, op1=ALU.add))
                done(V.tensor_copy(slot_rows[:], tabf[:, 2, :]))
                dve.wait_ge(row_full, 1)
                V.tensor_scalar(infor[:, 0, :], rowp[0:1, 0:128], float(NE - 1), None, ALU.min)
                done(V.tensor_scalar(infor[:, 3, :], rowp[0:1, 0:128], float(NE), None, ALU.is_lt))
                V.tensor_reduce(out=infor[:, 4, 0:1], in_=infor[:, 3, :].rearrange("o (g f) -> o g f", f=UN)[:, :, 0],
                                axis=AX.X, op=ALU.add)
                done(V.tensor_copy(infor[:, 1, :], rowp[0:1, 128:256]))
                V.memset(infor[:, 2, 0:1], 1.0)
                V.tensor_tensor(infor[:, 2, 1:128], infor[:, 1, 1:128], infor[:, 1, 0:127], ALU.not_equal)
                done(V.tensor_copy(infoi[:], infor[:, 1, :]))
                done(V.tensor_scalar(infoi[:], infoi[:], WBUF - 1, None, ALU.bitwise_and))
                si = slot_info[:].rearrange("o (s f) -> o s f", f=4)
                V.tensor_copy(si[:, :, 0], infor[:, 0, :])
                V.tensor_copy(si[:, :, 1], infor[:, 2, :])
                V.tensor_copy(si[:, :, 2], infoi[:])
                done(V.tensor_copy(si[:, :, 3], infor[:, 3, :]))
                V.tensor_copy(si[:, 127, 3:4], infor[:, 4, 0:1])

            @block.gpsimd
            def _(pool):
                P = nc.gpsimd
                pool.wait_ge(dve_step, 2)
                for k, part in enumerate(STATS):
                    r = slice(part[0], part[-1] + 1)
                    pool.wait_ge(var_ready, k + 1)
                    P.tensor_tensor(rstd[:, r], ve[:, r], mhalf[:].to_broadcast([128, len(part)]), ALU.pow).then_inc(rstd_ready, 1)
                pool.wait_ge(pos_ready, 1)
                for t in range(NT):
                    if t >= SB:
                        pool.wait_ge(table_used, t - SB + 1)
                    for k in range(4):
                        last = P.tensor_scalar(rowsel[:, t % SB, k, :], iota[:], posf[:, 1, t, k:k + 1], None, ALU.is_equal)
                    last.then_inc(rowsel_ready, 1)


def expert_stage(nc, T, slot_info, slot_rows):
    f32, i32 = mybir.dt.float32, mybir.dt.uint32
    ALU, ACT = mybir.AluOpType, mybir.ActivationFunctionType
    KC = DM // 128
    FC = FF // 128
    ITERS = SLOTS // UN
    WCOLS = KC * 2 * FF + FC * DM
    assert UN == WBUF and SLOTS % UN == 0

    with ExitStack() as ctx:
        sb = lambda name, shape, dt=f32: ctx.enter_context(nc.sbuf_tensor("ex_" + name, shape, dt))
        sem = lambda name: ctx.enter_context(nc.semaphore("ex_" + name))
        ident = sb("ident", [128, 128])
        wt = sb("wt", [128, WBUF * WCOLS])
        gidx = [sb(f"gidx{n}", [128, 1], i32) for n in range(4)]
        sidx = [sb(f"sidx{n}", [128, 1], i32) for n in range(2)]
        xg = [sb(f"xg{n}", [128, DM + NEXP]) for n in range(4)]
        share = sb("share", [128, 4])
        xT = [sb(f"xT{n}", [128, KC, 128]) for n in range(2)]
        gc = sb("gc", [128, FF])
        uc = sb("uc", [128, FF])
        sil = sb("sil", [128, FF])
        act_ = sb("act", [128, FF])
        actT = sb("actT", [128, FC, 128])
        ys = [sb(f"ys{n}", [128, DM]) for n in range(2)]
        pb = lambda name: ctx.enter_context(nc.psum_tensor("ex_" + name, [128, 512], f32))
        tx, ta = pb("tx"), pb("ta")
        gu = [pb(f"gu{n}") for n in range(2)]
        yb = [pb(f"y{n}") for n in range(2)]
        ident_ready = sem("ident_ready")
        w_ready = [sem(f"w_ready{n}") for n in range(2)]
        gathered = [sem(f"gathered{n}") for n in range(4)]
        scattered = [sem(f"scattered{n}") for n in range(2)]
        idx_ready, share_ready, sidx_ready, sent = (sem(n) for n in ("idx_ready", "share_ready", "sidx_ready", "sent"))
        tx_full, tx_taken = sem("tx_full"), sem("tx_taken")
        ta_full, ta_taken = sem("ta_full"), sem("ta_taken")
        gu_full, gate_ready, gu_taken, silu_ready, act_ready = (sem(n) for n in ("gu_full", "gate_ready", "gu_taken", "silu_ready", "act_ready"))
        y_full, y_ready = sem("y_full"), sem("y_ready")
        pe_turn, pool_turn, sp_turn = (sem(n) for n in ("pe_turn", "pool_turn", "sp_turn"))

        W_SEED, TX_SEED, GU_SEED, TA_SEED, Y_SEED, SENT_SEED = 4, 2, 1, 1, 2, 2

        def used(engine, it):
            return engine.If(engine.value_load(slot_info[0:1, bass.ds(it * (4 * UN) + 3, 1)], min_val=0, max_val=1))

        def turns(engine):
            return engine.value_load(slot_info[0:1, 4 * 127 + 3:4 * 128], min_val=1, max_val=ITERS)

        with nc.Block() as block:

            @block.sync
            def _(sp):
                sp.dma_start(ident[:], T["ident"]).then_inc(ident_ready, 16)

                def load(slot, n):
                    expert = sp.value_load(slot_info[0:1, bass.ds(slot * 4, 1)], min_val=0, max_val=NEXP - 1)
                    first = sp.value_load(slot_info[0:1, bass.ds(slot * 4 + 1, 1)], min_val=0, max_val=1)
                    buf = sp.value_load(slot_info[0:1, bass.ds(slot * 4 + 2, 1)], min_val=0, max_val=WBUF - 1)
                    sp.dma_start(wt[:, bass.ds(buf * WCOLS, WCOLS)],
                                 T["wexp"][bass.ds(expert, 1), :, :].rearrange("o p n -> p (o n)"),
                                 cond=first).then_inc(w_ready[n % 2], 16)

                load(0, 0)
                sp.sem_inc(y_full, W_SEED)
                with sp.Fori(0, ITERS) as it:
                    with used(sp, it):
                        for n in range(UN):
                            sp.wait_ge(y_full, it * UN + n - 2 + W_SEED)
                            sp.sem_inc(sp_turn, 1)
                            load(it * UN + n + 1, n + 1)
                            sp.wait_ge(w_ready[n % 2], (it * (UN // 2) + n // 2) * 16 + 16)
                            sp.sem_inc(sp_turn, 1)
                sp.wait_ge(w_ready[0], turns(sp) * (16 * UN // 2) + 16)
                sp.sem_inc(sp_turn, 1)

            @block.tensor
            def _(pe):
                M = nc.tensor.matmul

                def transpose_rows(n, count):
                    pe.wait_ge(tx_taken, count)
                    pe.sem_inc(pe_turn, 1)
                    for kc in range(KC):
                        last = nc.tensor.transpose(tx[:, 128 * kc:128 * kc + 128], xg[n % 4][:, 128 * kc:128 * kc + 128], ident[:])
                    last.then_inc(tx_full, 1)

                def weights(slot):
                    buf = pe.value_load(slot_info[0:1, bass.ds(slot * 4 + 2, 1)], min_val=0, max_val=WBUF - 1)
                    return pe.snap(buf * WCOLS)

                def gate_up(n, base, chunks):
                    for kc in chunks:
                        last = M(gu[n % 2][:], xT[n % 2][:, kc, :], wt[:, bass.ds(base + kc * 2 * FF, 2 * FF)],
                                 start=(kc == 0), stop=(kc == KC - 1))
                    if kc == KC - 1:
                        last.then_inc(gu_full, 1)

                pe.wait_ge(ident_ready, 16)
                pe.wait_ge(gathered[0], 16)
                transpose_rows(0, 2)
                pe.wait_ge(tx_taken, 3)
                pe.wait_ge(w_ready[0], 16)
                base = weights(0)
                gate_up(0, base, range(KC))
                pe.wait_ge(gathered[1], 16)
                transpose_rows(1, 3)
                with pe.Fori(0, ITERS) as it:
                    with used(pe, it):
                        base = weights(it * UN)
                        for n in range(UN):
                            s = it * UN + n
                            pe.wait_ge(gathered[(n + 2) % 4], (it + (n + 2) // 4) * 16 + 16)
                            transpose_rows(n + 2, s + 4)
                            pe.wait_ge(w_ready[(n + 1) % 2], (it * (UN // 2) + (n + 1) // 2) * 16 + 16)
                            pe.wait_ge(gu_taken, s + 1)
                            nxt = weights(s + 1)
                            gate_up(n + 1, nxt, range(KC // 2))
                            pe.wait_ge(act_ready, s + 1)
                            pe.wait_ge(ta_taken, s + 1)
                            pe.sem_inc(pe_turn, 1)
                            for c in range(FC):
                                last = nc.tensor.transpose(ta[:, 128 * c:128 * c + 128], act_[:, 128 * c:128 * c + 128], ident[:])
                            last.then_inc(ta_full, 1)
                            gate_up(n + 1, nxt, range(KC // 2, KC))
                            pe.wait_ge(ta_taken, s + 2)
                            pe.wait_ge(y_ready, s + 1)
                            for c in range(FC):
                                last = M(yb[n % 2][:], actT[:, c, :], wt[:, bass.ds(base + KC * 2 * FF + c * DM, DM)],
                                         start=(c == 0), stop=(c == FC - 1))
                            last.then_inc(y_full, 1)
                            base = nxt

            @block.scalar
            def _(act):
                A = nc.scalar
                act.sem_inc(ta_taken, TA_SEED)
                act.sem_inc(y_ready, Y_SEED)
                act.sem_inc(sent, SENT_SEED)
                with act.Fori(0, ITERS) as it:
                    with used(act, it):
                        for n in range(UN):
                            s = it * UN + n
                            act.wait_ge(gate_ready, s + 1)
                            A.activation(sil[:], gc[:], ACT.Silu).then_inc(silu_ready, 1)
                            act.wait_ge(ta_full, s + 1)
                            A.copy(actT[:].rearrange("p c t -> p (c t)"), ta[:, 0:FF]).then_inc(ta_taken, 1)
                            act.wait_ge(y_full, s + 1 + W_SEED)
                            act.wait_ge(sent, s + 1)
                            act.wait_ge(share_ready, s + 1)
                            A.activation(ys[n % 2][:], yb[n % 2][:], ACT.Copy, scale=share[:, n:n + 1]).then_inc(y_ready, 1)

            @block.vector
            def _(dve):
                V = nc.vector

                def take_rows(n, count):
                    dve.wait_ge(tx_full, count)
                    V.tensor_copy(xT[n % 2][:].rearrange("p k t -> p (k t)"), tx[:]).then_inc(tx_taken, 1)

                dve.sem_inc(tx_taken, TX_SEED)
                dve.sem_inc(gu_taken, GU_SEED)
                take_rows(0, 1)
                take_rows(1, 2)
                with dve.Fori(0, ITERS) as it:
                    with used(dve, it):
                        for n in range(UN):
                            s = it * UN + n
                            dve.wait_ge(gu_full, s + 1)
                            V.tensor_scalar(gc[:], gu[n % 2][:, 0:FF], -ALPHA, ALPHA, ALU.max, ALU.min).then_inc(gate_ready, 1)
                            V.tensor_scalar(uc[:], gu[n % 2][:, FF:2 * FF], -ALPHA, ALPHA, ALU.max, ALU.min).then_inc(gu_taken, 1)
                            dve.wait_ge(gu_taken, s + 2)
                            dve.wait_ge(silu_ready, s + 1)
                            V.tensor_tensor(act_[:], sil[:], uc[:], ALU.mult).then_inc(act_ready, 1)
                            take_rows(n + 2, s + 3)

            @block.gpsimd
            def _(pool):
                P = nc.gpsimd

                def gather(slot, n, count):
                    P.tensor_copy(gidx[n % 4][:], slot_rows[:, bass.ds(slot, 1)]).then_inc(idx_ready, 1)
                    pool.wait_ge(idx_ready, count + 1)
                    pool.sem_inc(pool_turn, 1)
                    P.indirect_dma_start(xg[n % 4][:], None, T["x2"], bass.IndirectOffsetOnAxis(ap=gidx[n % 4][:], axis=0)
                                         ).then_inc(gathered[n % 4], 16)

                def take_share(slot, n):
                    expert = pool.value_load(slot_info[0:1, bass.ds(slot * 4, 1)], min_val=0, max_val=NEXP - 1)
                    P.tensor_copy(share[:, n % 4:n % 4 + 1], xg[n % 4][:, bass.ds(expert + DM, 1)]).then_inc(share_ready, 1)

                def take_rows_index(slot, n):
                    P.tensor_copy(sidx[n % 2][:], slot_rows[:, bass.ds(slot, 1)]).then_inc(sidx_ready, 1)

                for n in range(4):
                    gather(n, n, n)
                for n in range(2):
                    pool.wait_ge(gathered[n], 16)
                    take_share(n, n)
                pool.wait_ge(tx_taken, 1 + TX_SEED)
                pool.wait_ge(share_ready, 1)
                gather(4, 0, 4)
                take_rows_index(0, 0)
                with pool.Fori(0, ITERS) as it:
                    with used(pool, it):
                        for n in range(UN):
                            s = it * UN + n
                            pool.wait_ge(sidx_ready, s + 1)
                            pool.wait_ge(y_ready, s + 1 + Y_SEED)
                            pool.sem_inc(pool_turn, 1)
                            P.indirect_dma_start(T["acc"], bass.IndirectOffsetOnAxis(ap=sidx[n % 2][:], axis=0), ys[n % 2][:],
                                                 None, compute_op=ALU.add).then_inc(scattered[n % 2], 16)
                            pool.wait_ge(tx_taken, s + 2 + TX_SEED)
                            pool.wait_ge(share_ready, s + 2)
                            pool.sem_inc(pool_turn, 1)
                            gather(s + 5, n + 1, s + 5)
                            pool.wait_ge(gathered[(n + 2) % 4], (it + (n + 2) // 4) * 16 + 16)
                            pool.sem_inc(pool_turn, 1)
                            take_share(s + 2, n + 2)
                            take_rows_index(s + 1, n + 1)
                            pool.wait_ge(scattered[n % 2], (it * (UN // 2) + n // 2) * 16 + 16)
                            pool.sem_inc(sent, 1)
                last = turns(pool)
                for n in range(4):
                    pool.wait_ge(gathered[n], last * 16 + (32 if n == 0 else 16))
                    pool.sem_inc(pool_turn, 1)


def output_stage(nc, T):
    with nc.semaphore("out_done") as out_done, nc.Block() as block:

        @block.sync
        def _(sp):
            for c in range(NCH):
                sp.dma_start(T["out"][c, 1:, :], T["acc"][256 * c:256 * c + 256, :]).then_inc(out_done, 16)
            sp.dma_start(T["out"][:, 0, :], T["acc"][256 * NCH:256 * NCH + NCH, :]).then_inc(out_done, 16)
            sp.wait_ge(out_done, 16 * (NCH + 1))


def build(nc, T):
    f32, u32, i32 = mybir.dt.float32, mybir.dt.uint32, mybir.dt.int32
    T["hs"] = nc.dram_tensor("ssm_rows", (128, 128, 64), f32).ap()
    T["x2"] = nc.dram_tensor("x2_rows", (TOKENS + 128, DM + NEXP), f32).ap()
    T["acc"] = nc.dram_tensor("acc_rows", (TOKENS + 128, DM), f32).ap()
    with ExitStack() as ctx:
        slot_info = ctx.enter_context(nc.sbuf_tensor("slot_info", [1, 4 * 128], i32))
        slot_rows = ctx.enter_context(nc.sbuf_tensor("slot_rows", [128, NS], u32))
        with nc.sbuf_tensor("H", [128, NT, DM], f32) as H:
            with ExitStack() as inputs_ctx:
                inputs, loads = attention_inputs(nc, inputs_ctx, T, H)
                ssm_stage(nc, T, loads)
                attention_stage(nc, T, H, inputs)
            route_stage(nc, T, H, slot_info, slot_rows)
        expert_stage(nc, T, slot_info, slot_rows)
        output_stage(nc, T)


def laid_out(x, cls_tok, L0_tok_log_dt, L0_tok_B_ri, L0_tok_inv_A_real, L0_tok_A_imag, L0_attn_c_attn_w, L0_attn_c_attn_b,
             L0_attn_c_proj_w, L0_attn_c_proj_b, L0_ffn_router_w, L0_ffn_expert_bias, L0_ffn_gate_w, L0_ffn_up_w,
             L0_ffn_down_w, L0_ffn_shared_gate_w, L0_ffn_shared_up_w, L0_ffn_shared_down_w):
    def chunks(a):
        return a.reshape(a.shape[0] // 128, 128, a.shape[1]).transpose(1, 0, 2)

    par = np.stack([L0_tok_inv_A_real, L0_tok_A_imag, L0_tok_B_ri[..., 0], L0_tok_B_ri[..., 1]])
    wt, b = chunks(L0_attn_c_attn_w.T), L0_attn_c_attn_b
    k, v = slice(DM, DM + HD), slice(DM + HD, DM + 2 * HD)
    selh = np.zeros((128, 4, 128), np.float32)
    for j in range(4):
        for m in range(4):
            selh[4 * j + m, m, 32 * j:32 * j + 32] = 1.0
    gu = np.concatenate([L0_ffn_gate_w, L0_ffn_up_w], axis=1)
    gu = gu.reshape(NEXP, 2 * FF, DM // 128, 128).transpose(0, 3, 2, 1).reshape(NEXP, 128, -1)
    dn = L0_ffn_down_w.reshape(NEXP, DM, FF // 128, 128).transpose(0, 3, 2, 1).reshape(NEXP, 128, -1)
    row, col = np.arange(128)[:, None], np.arange(128)[None, :]
    return {
        "ssm_par": par.reshape(4, 2, 128, 64).transpose(1, 3, 0, 2).reshape(128, 4, 128),
        "log_dt": L0_tok_log_dt.reshape(2, 128),
        "c_ri": x.reshape(NCH, 2, 128, 64, 2).transpose(1, 3, 4, 2, 0).reshape(128, 2, 128 * NCH),
        "watt": np.concatenate([wt[:, :, 0:DM]] + [wt[:, :, k]] * 4 + [wt[:, :, v]] * 4, axis=2),
        "battn": np.concatenate([b[:DM].reshape(4, 128).T, np.tile(b[k], 4)[:, None], np.tile(b[v], 4)[:, None]], axis=1),
        "wo": chunks(L0_attn_c_proj_w.T),
        "bo": L0_attn_c_proj_b.reshape(1, DM),
        "cls": cls_tok.reshape(1, DM),
        "selh": selh,
        "quad": (row // 32 == np.arange(4)).astype(np.float32),
        "selv": np.roll(selh, 32, axis=0),
        "mask": np.where(col <= row, 0.0, -3e38).astype(np.float32),
        "ident": np.eye(128, dtype=np.float32),
        "upper": (row < col).astype(np.float32),
        "iota": np.broadcast_to(col, (128, 128)).astype(np.float32),
        "rowid": row.astype(np.float32),
        "isrow": (row < NCH).astype(np.float32),
        "router": chunks(L0_ffn_router_w.T),
        "ebias": L0_ffn_expert_bias.reshape(1, NEXP),
        "sgu": chunks(np.concatenate([L0_ffn_shared_gate_w, L0_ffn_shared_up_w], axis=0).T),
        "sdn": chunks(L0_ffn_shared_down_w.T),
        "wexp": np.concatenate([gu, dn], axis=2),
    }


def kernel(**inputs):
    import concourse.bacc as bacc
    from concourse.bass_utils import run_bass_kernel_spmd

    arrays = {f"in_{n}_dram": np.ascontiguousarray(a) for n, a in laid_out(**{n: np.asarray(a) for n, a in inputs.items()}).items()}
    nc = bacc.Bacc("TRN2", target_bir_lowering=False, num_devices=1)
    T = {n[3:-5]: nc.dram_tensor(n, a.shape, mybir.dt.from_np(a.dtype), kind="ExternalInput").ap() for n, a in arrays.items()}
    T["out"] = nc.dram_tensor("out_dram", (NCH, 1 + 256, DM), mybir.dt.float32, kind="ExternalOutput").ap()
    build(nc, T)
    r = run_bass_kernel_spmd(nc, [arrays], core_ids=[0])
    return r.results[0]["out_dram"]
```
